# Optimizing a Trainium2 kernel written in Bass

```python
import numpy as np
import jax
import jax.numpy as jnp

def _softmax(x, axis=-1):
    return jax.nn.softmax(x, axis=axis)

def _gelu(x):
    return jax.nn.gelu(x, approximate=True)

def _silu(x):
    return jax.nn.silu(x)

def _sigmoid(x):
    return jax.nn.sigmoid(x)

def _layernorm(x, axis=-1, eps=1e-05):
    m = jnp.mean(x, axis=axis, keepdims=True)
    v = jnp.var(x, axis=axis, keepdims=True)
    return (x - m) / jnp.sqrt(v + eps)

def _scatter_add(tgt, idx, src, axis=0):
    return tgt.at[idx].add(src)

def _segment_sum(src, seg, n):
    return jax.ops.segment_sum(src, seg, n)
kernel_name = 'mk_flamingo_gated_d1_seqx_r8_aecfd0'

def setup_inputs(seed: int=0):
    np.random.seed(seed)
    _w = jnp.asarray

    def _rec_inputs():
        import jax
        import jax.numpy as jnp
        _rk = jax.random.key(seed)
        x = -0.0003929 + 0.9999 * jax.random.normal(jax.random.fold_in(_rk, 1), (32, 56, 256), jnp.float32)
        _lenS = 56 - jax.random.randint(jax.random.fold_in(_rk, 7), (32,), 0, max(1, 56 // 4) + 1, jnp.int32)
        _lenS2 = 1500 - jax.random.randint(jax.random.fold_in(_rk, 8), (32,), 0, max(1, 1500 // 4) + 1, jnp.int32)
        _ctx_2048P = jax.random.normal(jax.random.fold_in(_rk, 11), (32, 16, 256), jnp.float32)
        _ctx_2048c = jax.random.dirichlet(jax.random.fold_in(_rk, 511), 0.3 * jnp.ones((16,), jnp.float32), (32, 1500))
        _ctx_2048t = jnp.einsum('bsk,bkd->bsd', _ctx_2048c, _ctx_2048P)
        _ctx_2048t = _ctx_2048t * jax.lax.rsqrt(jnp.mean(jnp.square(_ctx_2048t)) + 1e-12) * 0.953939
        ctx_2048 = -0.000514642 + 1.00011 * (_ctx_2048t + 0.3 * jax.random.normal(jax.random.fold_in(_rk, 611), (32, 1500, 256), jnp.float32))
        _validS = jnp.arange(56)[None, :] < _lenS[:, None]
        _validS2 = jnp.arange(1500)[None, :] < _lenS2[:, None]
        _causal = jnp.tril(jnp.ones((56, 56), dtype=bool))
        mask_BxS2_ik0 = jnp.where(jnp.broadcast_to(_validS2[:, :], (32, 1500)), 0, 1).astype(jnp.int32)
        _g = jax.random.normal(jax.random.fold_in(_rk, 9001), (2, 1), jnp.float32)
        _g = jnp.sign(_g) * jnp.maximum(jnp.abs(_g), 1.0) + (_g == 0) * 1.0
        g_xattn = _g[0]
        g_ffn = _g[1]
        return (x, ctx_2048, mask_BxS2_ik0, g_xattn, g_ffn)
    x, ctx_2048, mask_BxS2_ik0, g_xattn, g_ffn = _rec_inputs()

    def _L0_xattn_setup():
        import jax, jax.numpy as jnp
        import numpy as np
        import math
        H = 256
        NH = 16
        HD = H // NH
        EPS_LN = 1e-05
        RES_SCALE_MAX = 0.3

        def _nan_clean(x, lim=10000.0):
            return jnp.nan_to_num(x, nan=0.0, posinf=lim, neginf=-lim)
        key = jax.random.key(seed)
        ks = jax.random.split(key, 12)
        B, S, T = (4, 256, 32)
        std = 1.0 / math.sqrt(H)
        return {'hidden_states': jax.random.normal(ks[0], (B, S, H), jnp.float32), 'audio_tokens': jax.random.normal(ks[1], (B, T, H), jnp.float32), 'attention_mask': jax.random.randint(ks[2], (B, T), 0, 2, jnp.int32), 'Wq': jax.random.normal(ks[3], (H, H), jnp.float32) * std, 'bq': jnp.zeros((H,), jnp.float32), 'Wk': jax.random.normal(ks[4], (H, H), jnp.float32) * std, 'bk': jnp.zeros((H,), jnp.float32), 'Wv': jax.random.normal(ks[5], (H, H), jnp.float32) * std, 'bv': jnp.zeros((H,), jnp.float32), 'Wo': jax.random.normal(ks[6], (H, H), jnp.float32) * std, 'bo': jnp.zeros((H,), jnp.float32), 'ln_gamma': jnp.ones((H,), jnp.float32), 'ln_beta': jnp.zeros((H,), jnp.float32), 'residual_scale': jnp.float32(0.05)}
    _L0_xattn_all = _L0_xattn_setup()
    _L0_xattn_in = {k: v for k, v in _L0_xattn_all.items() if k in ('Wq', 'bq', 'Wk', 'bk', 'Wv', 'bv', 'Wo', 'bo', 'ln_gamma', 'ln_beta', 'residual_scale')}
    del _L0_xattn_all

    def _L0_ffn_setup():
        import jax, jax.numpy as jnp
        import numpy as np
        NUM_EXPERTS = 8
        TOP_K = 2
        key = jax.random.key(seed)
        k1, k2, k3, k4 = jax.random.split(key, 4)
        B, T, C, E, D = (4, 256, 256, NUM_EXPERTS, 256)
        scale = 0.02
        return {'x': jax.random.normal(k1, (B, T, C), dtype=jnp.float32), 'w_router': jax.random.normal(k2, (C, E), dtype=jnp.float32) * scale, 'w_fc': jax.random.normal(k3, (E, C, D), dtype=jnp.float32) * scale, 'w_proj': jax.random.normal(k4, (E, D, C), dtype=jnp.float32) * scale}
    _L0_ffn_all = _L0_ffn_setup()
    _L0_ffn_in = {k: v for k, v in _L0_ffn_all.items() if k in ('w_router', 'w_fc', 'w_proj')}
    del _L0_ffn_all
    return {'x': x, 'ctx_2048': ctx_2048, 'mask_BxS2_ik0': mask_BxS2_ik0, 'g_xattn': g_xattn, 'g_ffn': g_ffn, 'L0_xattn_Wq': _L0_xattn_in['Wq'], 'L0_xattn_bq': _L0_xattn_in['bq'], 'L0_xattn_Wk': _L0_xattn_in['Wk'], 'L0_xattn_bk': _L0_xattn_in['bk'], 'L0_xattn_Wv': _L0_xattn_in['Wv'], 'L0_xattn_bv': _L0_xattn_in['bv'], 'L0_xattn_Wo': _L0_xattn_in['Wo'], 'L0_xattn_bo': _L0_xattn_in['bo'], 'L0_xattn_ln_gamma': _L0_xattn_in['ln_gamma'], 'L0_xattn_ln_beta': _L0_xattn_in['ln_beta'], 'L0_xattn_residual_scale': _L0_xattn_in['residual_scale'], 'L0_ffn_w_router': _L0_ffn_in['w_router'], 'L0_ffn_w_fc': _L0_ffn_in['w_fc'], 'L0_ffn_w_proj': _L0_ffn_in['w_proj']}

def reference(x, ctx_2048, mask_BxS2_ik0, g_xattn, g_ffn, L0_xattn_Wq, L0_xattn_bq, L0_xattn_Wk, L0_xattn_bk, L0_xattn_Wv, L0_xattn_bv, L0_xattn_Wo, L0_xattn_bo, L0_xattn_ln_gamma, L0_xattn_ln_beta, L0_xattn_residual_scale, L0_ffn_w_router, L0_ffn_w_fc, L0_ffn_w_proj):
    import jax
    import jax.numpy as jnp

    def _L0_xattn_ref(hidden_states, audio_tokens, attention_mask, Wq, bq, Wk, bk, Wv, bv, Wo, bo, ln_gamma, ln_beta, residual_scale):
        import jax, jax.numpy as jnp
        import numpy as np
        import math
        H = 256
        NH = 16
        HD = H // NH
        EPS_LN = 1e-05
        RES_SCALE_MAX = 0.3

        def _nan_clean(x, lim=10000.0):
            return jnp.nan_to_num(x, nan=0.0, posinf=lim, neginf=-lim)
        B, S, _ = hidden_states.shape
        T = audio_tokens.shape[1]
        hs = _nan_clean(hidden_states).astype(jnp.float32)
        at = _nan_clean(audio_tokens).astype(jnp.float32)

        def proj(x, W, b, L):
            y = x @ W.T + b
            return y.reshape(B, L, NH, HD).transpose(0, 2, 1, 3)
        q = _nan_clean(proj(hs, Wq, bq, S))
        k = _nan_clean(proj(at, Wk, bk, T))
        v = _nan_clean(proj(at, Wv, bv, T))
        scale = max(math.sqrt(HD), 1e-08)
        scores = jnp.einsum('bhsd,bhtd->bhst', q, k) / scale
        scores = jnp.clip(scores, -50.0, 50.0)
        scores = jnp.nan_to_num(scores, nan=0.0, posinf=50.0, neginf=-50.0)
        attend = (attention_mask.astype(jnp.float32) > 0.5)[:, None, None, :]
        scores = jnp.where(attend, scores, -10000.0)
        scores = jnp.clip(scores, -50.0, 50.0)
        probs = jax.nn.softmax(scores, axis=-1)
        probs = jnp.nan_to_num(probs, nan=0.0, posinf=1.0, neginf=0.0)
        probs = probs / (probs.sum(axis=-1, keepdims=True) + 1e-08)
        ctx = jnp.einsum('bhst,bhtd->bhsd', probs, v)
        ctx = ctx.transpose(0, 2, 1, 3).reshape(B, S, H)
        delta = _nan_clean(ctx @ Wo.T + bo)
        rs = jnp.clip(residual_scale, 0.0, RES_SCALE_MAX)
        delta = rs * delta
        mu = delta.mean(axis=-1, keepdims=True)
        var = jnp.mean((delta - mu) ** 2, axis=-1, keepdims=True)
        delta = (delta - mu) / jnp.sqrt(var + EPS_LN) * ln_gamma + ln_beta
        return delta

    def _L0_ffn_ref(x, w_router, w_fc, w_proj):
        import jax, jax.numpy as jnp
        import numpy as np
        NUM_EXPERTS = 8
        TOP_K = 2
        B, T, C = x.shape
        E = w_fc.shape[0]
        x_flat = x.reshape(-1, C)
        N = x_flat.shape[0]
        router_logits = x_flat @ w_router
        top_vals, top_idx = jax.lax.top_k(router_logits, TOP_K)
        probs = jax.nn.softmax(top_vals, axis=-1)
        rows = jnp.arange(N)[:, None]
        w_tok = jnp.zeros((N, E), dtype=x.dtype).at[rows, top_idx].add(probs)
        h = jnp.einsum('nc,ecd->ned', x_flat, w_fc)
        h = jnp.square(jax.nn.relu(h))
        y = jnp.einsum('ned,edc->nec', h, w_proj)
        out = jnp.einsum('nec,ne->nc', y, w_tok)
        return out.reshape(B, T, C)
    x = x + jnp.tanh(g_xattn[0]) * _L0_xattn_ref(_layernorm(x, axis=-1), ctx_2048, mask_BxS2_ik0, L0_xattn_Wq, L0_xattn_bq, L0_xattn_Wk, L0_xattn_bk, L0_xattn_Wv, L0_xattn_bv, L0_xattn_Wo, L0_xattn_bo, L0_xattn_ln_gamma, L0_xattn_ln_beta, L0_xattn_residual_scale)
    x = x + jnp.tanh(g_ffn[0]) * _L0_ffn_ref(_layernorm(x, axis=-1), L0_ffn_w_router, L0_ffn_w_fc, L0_ffn_w_proj)
    return x

_drawn_inputs = setup_inputs


def setup_inputs(seed=0):
    import zlib

    import numpy as np

    out = dict(_drawn_inputs(seed))
    spreads = {'L0_xattn_bq': (0.0, 0.299),
     'L0_xattn_bk': (0.0, 0.8),
     'L0_xattn_bv': (0.0, 0.1),
     'L0_xattn_bo': (0.0, 0.1),
     'L0_xattn_ln_gamma': (1.0, 0.2),
     'L0_xattn_ln_beta': (0.0, 0.1)}
    factors = {'L0_ffn_w_router': 3.12, 'L0_ffn_w_fc': 2.95, 'L0_ffn_w_proj': 2.683}
    for name, (base, spread) in spreads.items():
        noise = np.random.default_rng([zlib.crc32(name.encode()), seed]).standard_normal(out[name].shape)
        drawn = base * np.exp(spread * noise) if base else spread * noise
        out[name] = jnp.asarray(drawn.astype(out[name].dtype))
    for name, factor in factors.items():
        out[name] = (out[name] * factor).astype(out[name].dtype)
    return out
```

```python
import concourse.bass as bass
from concourse import mybir
from contextlib import ExitStack

B, S, D, T = 32, 56, 256, 1500
NH, HD = 16, 16
P = 128
KD = D // P
TC = 125
GC = 4
TG = TC * GC
NG = T // TG
NC = NG * GC
TOK = B * S
NT = TOK // P
ST = 4
HS = NH // ST
HW = HS * HD
QW = 448
NQ = TOK // QW
NE = 8
FT = 256
NF = TOK // FT
VW = 32
NB = 4
EPS = 1e-5
CLIP = 50.0
EXP_HI = 5.184705528587072e21
EXP_LO = 1.9287498479639178e-22
BIG = 3.0e38
SCALE = HD ** -0.5
RES_SCALE_MAX = 0.3


def gated_cross_attention_moe(nc, a, out):
    fp32, fp32r, i32 = mybir.dt.float32, mybir.dt.float32r, mybir.dt.int32
    ALU = mybir.AluOpType
    ACT = mybir.ActivationFunctionType
    AX = mybir.AxisListType

    with ExitStack() as ctx:
        def sem(name):
            return ctx.enter_context(nc.semaphore(name))

        def sb(name, shape, dt=fp32, scope=ctx):
            return scope.enter_context(nc.sbuf_tensor(name, shape, dt))

        def plain(ap):
            return ap.bitcast(fp32)

        def wait(eng, s, value):
            if not isinstance(value, int) or value > 0:
                eng.wait_ge(s, value)

        x_sb = sb("x_sb", [P, NT, D])
        ctxo = sb("ctxo", [P, ST, TOK])
        wo = sb("wo", [P, ST, D])
        wr = sb("wr", [P, KD, NE])
        bo = sb("bo", [P, D])
        gam = sb("gam", [P, D])
        bet = sb("bet", [P, D])
        ident = sb("ident", [P, P])
        sumsel = sb("sumsel", [P, P])
        gates = sb("gates", [P, 3])
        tg = sb("tg", [P, 2])
        rs = sb("rs", [P, 1])
        st6 = sb("st6", [P, NT, 6])
        mv = sb("mv", [P, NT, 2])
        var_e = sb("var_e", [P, NT])
        std = sb("std", [P, NT])
        rstd = sb("rstd", [P, NT])
        rev_e = sb("rev_e", [P, NE])

        att = ExitStack()
        xn = sb("xn", [P, 2, D], scope=att)
        wk = sb("wk", [P, KD, D], scope=att)
        wv = sb("wv", [P, KD, D], scope=att)
        wq = sb("wq", [P, KD, D], scope=att)
        wk_hi = sb("wk_hi", [P, KD, D], fp32r, scope=att)
        wk_lo = sb("wk_lo", [P, KD, D], fp32r, scope=att)
        wv_hi = sb("wv_hi", [P, KD, D], fp32r, scope=att)
        wv_lo = sb("wv_lo", [P, KD, D], fp32r, scope=att)
        wq2 = sb("wq2", [P, KD, ST, 2, HW], scope=att)
        bq2 = sb("bq2", [P, ST], scope=att)
        bk = sb("bk", [P, KD], scope=att)
        bv = sb("bv", [P, D], scope=att)
        hmask = sb("hmask", [P, HS], scope=att)
        mask_i = sb("mask_i", [P, B * NC], i32, scope=att)
        m_scale = sb("m_scale", [P, B * NC], scope=att)
        one = sb("one", [P, KD], scope=att)
        m_bias = sb("m_bias", [P, B * NC], scope=att)
        qT = sb("qT", [P, ST, TOK], scope=att)
        raw = sb("raw", [P, 3, KD, TG], scope=att)
        c_hi = sb("c_hi", [P, 2, KD, TG], fp32r, scope=att)
        c_lo = sb("c_lo", [P, 2, KD, TG], fp32r, scope=att)
        kst = sb("kst", [P, 2, ST, TG], fp32r, scope=att)
        vst = sb("vst", [P, 2, GC, NH, VW], scope=att)
        prob = sb("prob", [P, 3, NH * S], scope=att)
        q_rnd = sb("q_rnd", [P, ST, S], fp32r, scope=att)
        q_rem = sb("q_rem", [P, ST, S], scope=att)
        q_hi = sb("q_hi", [P, 2, ST, HS, S], fp32r, scope=att)
        q_lo = sb("q_lo", [P, 2, ST, HS, S], fp32r, scope=att)
        att.close()

        post = ExitStack()
        rec = sb("rec", [P, 2, QW], scope=post)
        dlt = sb("dlt", [P, NT, D], scope=post)
        yT_hi = sb("yT_hi", [P, KD, TOK], fp32r, scope=post)
        yT_lo = sb("yT_lo", [P, KD, TOK], fp32r, scope=post)
        wr_hi = sb("wr_hi", [P, KD, NE], fp32r, scope=post)
        wr_lo = sb("wr_lo", [P, KD, NE], fp32r, scope=post)
        w_raw = sb("w_raw", [P, 2, 2, KD, D], scope=post)
        wf_hi = sb("wf_hi", [P, NE, KD, D], fp32r, scope=post)
        wf_lo = sb("wf_lo", [P, NE, KD, D], fp32r, scope=post)
        wp_hi = sb("wp_hi", [P, NE, KD, D], fp32r, scope=post)
        wp_lo = sb("wp_lo", [P, NE, KD, D], fp32r, scope=post)
        logit = sb("logit", [P, NT, NE], scope=post)
        hit = sb("hit", [P, NT, NE], scope=post)
        pick1 = sb("pick1", [P, NT, NE], scope=post)
        pick2 = sb("pick2", [P, NT, NE], scope=post)
        w_tok = sb("w_tok", [P, NT, NE], scope=post)
        top1 = sb("top1", [P, NT], scope=post)
        top2 = sb("top2", [P, NT], scope=post)
        firstof = sb("firstof", [P, NT], scope=post)
        e21 = sb("e21", [P, NT], scope=post)
        pr1 = sb("pr1", [P, NT], scope=post)
        pr2 = sb("pr2", [P, NT], scope=post)
        h_relu = sb("h_relu", [P, 2, KD, FT], scope=post)
        h_sq = sb("h_sq", [P, 2, KD, FT], scope=post)
        h_hi = sb("h_hi", [P, NB, KD, FT], fp32r, scope=post)
        h_lo = sb("h_lo", [P, NB, KD, FT], fp32r, scope=post)
        post.close()

        xnT = ctxo[:, 0:KD, :]

        sc_ps = ctx.enter_context(nc.psum_tensor("sc_ps", [P, 4, 512], fp32))
        k_ps = ctx.enter_context(nc.psum_tensor("k_ps", [P, KD, 512], fp32))
        v_ps = ctx.enter_context(nc.psum_tensor("v_ps", [P, 512], fp32))
        o_ps = ctx.enter_context(nc.psum_tensor("o_ps", [P, 512], fp32))
        spare_ps = [k_ps[:, 0, :], k_ps[:, 1, :], v_ps[:, :], o_ps[:, :]]

        x_in = sem("x_in")
        w_in = sem("w_in")
        post_in = sem("post_in")
        v_ones = sem("v_ones")
        w_split = sem("w_split")
        m_ready = sem("m_ready")
        std_done = sem("std_done")
        var_done = sem("var_done")
        xn_done = sem("xn_done")
        xt_done = sem("xt_done")
        xT_done = sem("xT_done")
        qp_done = sem("qp_done")
        qT_done = sem("qT_done")
        tanh_done = sem("tanh_done")
        x_shift = sem("x_shift")
        raw_in = [sem(f"raw_in{i}") for i in range(3)]
        ctx_hi = sem("ctx_hi")
        ctx_split = sem("ctx_split")
        kproj_done = sem("kproj_done")
        vproj_done = sem("vproj_done")
        k_hi = sem("k_hi")
        k_lo = sem("k_lo")
        v_evac = sem("v_evac")
        q_ready = sem("q_ready")
        q_step = sem("q_step")
        scores_done = sem("scores_done")
        exp_done = sem("exp_done")
        clip_done = sem("clip_done")
        pv_done = sem("pv_done")
        o_evac = sem("o_evac")
        sum_done = sem("sum_done")
        rec_done = sem("rec_done")
        norm_done = sem("norm_done")
        op_done = sem("op_done")
        dlt_evac = sem("dlt_evac")
        wr_split = sem("wr_split")
        dlt_done = sem("dlt_done")
        x1_done = sem("x1_done")
        y_done = sem("y_done")
        yt_done = sem("yt_done")
        yhi_done = sem("yhi_done")
        ylo_done = sem("ylo_done")
        lg_done = sem("lg_done")
        diff_done = sem("diff_done")
        e21_done = sem("e21_done")
        wraw_in = [sem(f"wraw_in{i}") for i in range(2)]
        we_hi = sem("we_hi")
        we_lo = sem("we_lo")
        fc_done = sem("fc_done")
        relu_done = sem("relu_done")
        sq_done = sem("sq_done")
        hhi_done = sem("hhi_done")
        hlo_done = sem("hlo_done")
        y2_done = sem("y2_done")
        acc_done = sem("acc_done")
        out_done = sem("out_done")
        dve_seq = sem("dve_seq")
        pool_seq = sem("pool_seq")

        N_X, N_W, N_POST = 2, 11, 7

        block = ctx.enter_context(nc.Block())

        def bcast(ap, n):
            return ap.partition_broadcast(n)

        @block.sync
        def _(sp):
            sp.dma_start(x_sb[:, :, :], a["x"]).then_inc(x_in, 16)
            sp.dma_start(ident[:, :], a["ident"]).then_inc(x_in, 16)
            for dst, src in ((wk, "wk"), (wv, "wv"), (wq, "wq")):
                sp.dma_start(dst[:, :, :], a[src]).then_inc(w_in, 16)
            sp.dma_start(bk[:, :], a["bk"]).then_inc(w_in, 16)
            sp.dma_start(bq2[:, :], a["bq2"]).then_inc(w_in, 16)
            sp.dma_start(bv[:, :], bcast(a["bv"], P)).then_inc(w_in, 16)
            sp.dma_start(hmask[:, :], a["hmask"]).then_inc(w_in, 16)
            sp.dma_start(mask_i[0:TC, :], a["mask"]).then_inc(w_in, 16)
            sp.dma_start(gates[:, 0:1], bcast(a["g_xattn"], P)).then_inc(w_in, 16)
            sp.dma_start(gates[:, 1:2], bcast(a["g_ffn"], P)).then_inc(w_in, 16)
            sp.dma_start(bet[:, :], bcast(a["beta"], P)).then_inc(w_in, 16)
            for g in range(3):
                sp.dma_start(raw[:, g, :, :], a["ctxT"][0, g]).then_inc(raw_in[g], 16)
            for dst, src in ((wo, "wo"), (wr, "wr")):
                sp.dma_start(dst[:, :, :], a[src]).then_inc(post_in, 16)
            for dst, src in ((sumsel, "sumsel"), (rev_e, "rev_e")):
                sp.dma_start(dst[:, :], a[src]).then_inc(post_in, 16)
            for dst, src in ((bo, "bo"), (gam, "gamma")):
                sp.dma_start(dst[:, :], bcast(a[src], P)).then_inc(post_in, 16)
            sp.dma_start(gates[:, 2:3], bcast(a["rscale"], P)).then_inc(post_in, 16)
            with sp.Fori(1, B) as b:
                for g in range(NG):
                    sp.wait_ge(ctx_split, b * NG + g - 2)
                    sp.dma_start(raw[:, g, :, :], a["ctxT"][bass.ds(b, 1), g].squeeze(0)).then_inc(raw_in[g], 16)
            sp.wait_ge(pv_done, B * NC)
            for e in range(NE):
                if e >= 2:
                    sp.wait_ge(we_lo, 2 * (e - 1))
                sp.dma_start(w_raw[:, e % 2, 0, :, :], a["wf"][e]).then_inc(wraw_in[e % 2], 16)
                sp.dma_start(w_raw[:, e % 2, 1, :, :], a["wp"][e]).then_inc(wraw_in[e % 2], 16)
            for f in range(NF):
                sp.wait_ge(acc_done, 2 * NE * (f + 1))
                sp.dma_start(out[:, 2 * f:2 * f + 2, :], x_sb[:, 2 * f:2 * f + 2, :]).then_inc(out_done, 16)
            sp.wait_ge(out_done, 16 * NF)

        @block.gpsimd
        def _(pool):
            pool.memset(one[:, :], 1.0).then_inc(pool_seq, 1)
            pool.wait_ge(pool_seq, 1)
            pool.memset(vst[:, :, :, :, HD:VW], 1.0).then_inc(v_ones, 1)

            def split(b, g, par):
                n = b * NG + g
                s = (par + g) % 2
                pool.wait_ge(raw_in[g], 16 * b + 16)
                wait(pool, vproj_done, GC * (n - 1))
                r = raw[:, g, :, :]
                pool.tensor_tensor(c_hi[:, s, :, :], r, one[:, :].unsqueeze(2).to_broadcast([P, KD, TG]),
                                   ALU.mult).then_inc(ctx_hi, 1)
                pool.wait_ge(ctx_hi, n + 1)
                pool.tensor_tensor(c_lo[:, s, :, :], raw[:, g, :, :], plain(c_hi[:, s, :, :]),
                                   ALU.subtract).then_inc(ctx_split, 1)

            for g in range(NG):
                split(0, g, 0)
            for g in range(NG):
                split(1, g, 1)
            pool.wait_ge(tanh_done, 1)
            pool.wait_ge(xn_done, NT)
            pool.tensor_scalar(bet[:, :], bet[:, :], tg[:, 0:1], None, ALU.mult).then_inc(pool_seq, 1)
            pool.wait_ge(pool_seq, 2)
            for t in range(NT):
                pool.tensor_tensor(x_sb[:, t, :], x_sb[:, t, :], bet[:, :], ALU.add).then_inc(x_shift, 1)
            with pool.Fori(1, B // 2) as i:
                for par in range(2):
                    for g in range(NG):
                        split(2 * i + par, g, par)
            for u in range(NQ * ST):
                q, g = divmod(u, ST)
                cols = slice(q * QW, (q + 1) * QW)
                pool.wait_ge(rec_done, u + 1)
                pool.tensor_tensor(ctxo[:, g, cols], ctxo[:, g, cols], rec[:, u % 2, :], ALU.mult).then_inc(norm_done, 1)
            pool.wait_ge(x_shift, NT)
            for t in range(NT):
                pool.wait_ge(dlt_done, t + 1)
                pool.tensor_tensor(dlt[:, t, :], dlt[:, t, :], gam[:, :], ALU.mult).then_inc(pool_seq, 1)
                pool.wait_ge(pool_seq, t + 3)
                pool.tensor_tensor(x_sb[:, t, :], x_sb[:, t, :], dlt[:, t, :], ALU.add).then_inc(x1_done, 1)
            with pool.Fori(0, NF) as f:
                for e in range(NE):
                    pool.wait_ge(hhi_done, f * NE + e + 1)
                    pool.tensor_tensor(h_lo[:, e % NB, :, :], h_sq[:, e % 2, :, :], plain(h_hi[:, e % NB, :, :]),
                                       ALU.subtract).then_inc(hlo_done, 1)

        @block.tensor
        def _(pe):
            def mm3(ps, w_h, w_l, m_h, m_l, first, last):
                pe.matmul(ps, w_h, m_h, start=first, stop=False)
                pe.matmul(ps, w_h, m_l, start=False, stop=False)
                return pe.matmul(ps, w_l, m_h, start=False, stop=last)

            pe.wait_ge(x_in, 16 * N_X)
            for t in range(NT):
                pe.wait_ge(xn_done, t + 1)
                wait(pe, xT_done, t - 3)
                for k in range(KD):
                    last = pe.transpose(sc_ps[:, t % 4, k * P:(k + 1) * P], xn[:, t % 2, k * P:(k + 1) * P], ident[:, :])
                last.then_inc(xt_done, 1)

            def k_proj(n, m, s):
                wait(pe, ctx_split, n + 1)
                wait(pe, k_lo, 4 * n - 4 + 2 * m + 2)
                wait(pe, k_hi, 4 * n - 4 + 2 * m + 2)
                ws = slice(m * P, (m + 1) * P)
                for k in range(KD):
                    last = mm3(k_ps[:, m, 0:TG], wk_hi[:, k, ws], wk_lo[:, k, ws], c_hi[:, s, k, :], c_lo[:, s, k, :],
                               k == 0, k == KD - 1)
                last.then_inc(kproj_done, 1)

            def v_proj(n, j, s):
                wait(pe, v_evac, n * GC + j)
                cs = slice(j * TC, (j + 1) * TC)
                for k in range(KD):
                    last = mm3(v_ps[0:TC, 0:D], c_hi[:, s, k, cs], c_lo[:, s, k, cs], wv_hi[:, k, :], wv_lo[:, k, :],
                               k == 0, k == KD - 1)
                last.then_inc(vproj_done, 1)

            def scores(b, j, par, s):
                n = b * NC + j
                if j == 0:
                    pe.wait_ge(q_ready, 2 * b + 2)
                if j % GC == 0:
                    pe.wait_ge(k_lo, 4 * (b * NG + j // GC + 1))
                wait(pe, exp_done, n - 1)
                cs = slice(j % GC * TC, (j % GC + 1) * TC)
                for i in range(ST):
                    ps = sc_ps[0:TC, 2 * (j % 2) + i // 2, i % 2 * HS * S:(i % 2 + 1) * HS * S]
                    k = kst[:, s, i, cs]
                    pe.matmul(ps, k, q_hi[:, par, i, :, :], start=True, stop=False)
                    last = pe.matmul(ps, k, q_lo[:, par, i, :, :], start=False, stop=True)
                last.then_inc(scores_done, 1)

            def pv(b, j, par, s):
                n = b * NC + j
                if j == 0:
                    wait(pe, o_evac, b)
                pe.wait_ge(v_evac, n + 1)
                pe.wait_ge(clip_done, n + 1)
                for h in range(NH):
                    c, q = divmod(h, ST)
                    last = pe.matmul(o_ps[q * 32:q * 32 + VW, c * S:(c + 1) * S], vst[0:TC, s, j % GC, h, :],
                                     prob[0:TC, j % 3, h * S:(h + 1) * S], start=(j == 0 and c == 0),
                                     stop=(j == NC - 1), skip_group_check=True)
                last.then_inc(pv_done, 1)

            def batch(b, par, first=False, final=False):
                for j in range(NC):
                    g = j // GC
                    n, s = b * NG + g, (par + g) % 2
                    scores(b, j, par, s)
                    if not (final and g == NG - 1):
                        if j % GC < KD:
                            k_proj(n + 1, j % GC, 1 - s)
                        v_proj(n + 1, j % GC, 1 - s)
                    if j > 0:
                        pv(b, j - 1, par, (par + (j - 1) // GC) % 2)
                    elif not first:
                        pv(b - 1, NC - 1, 1 - par, 1 - s)

            pe.wait_ge(w_split, 4)
            for m in range(KD):
                k_proj(0, m, 0)
            for j in range(GC):
                v_proj(0, j, 0)
            pe.wait_ge(w_split, 6)
            for u in range(NQ * ST):
                q, i = divmod(u, ST)
                wait(pe, xT_done, NT)
                wait(pe, qT_done, u - 3)
                for k in range(KD):
                    last = pe.matmul(sc_ps[:, u % 4, 0:QW], wq2[:, k, i, :, :], xnT[:, k, q * QW:(q + 1) * QW],
                                     start=(k == 0), stop=(k == KD - 1))
                last.then_inc(qp_done, 1)
            pe.wait_ge(qT_done, NQ * ST)
            batch(0, 0, first=True)
            batch(1, 1)
            with pe.Fori(1, B // 2 - 1) as i:
                batch(2 * i, 0)
                batch(2 * i + 1, 1)
            batch(B - 2, 0)
            batch(B - 1, 1, final=True)
            pv(B - 1, NC - 1, 1, (1 + NG - 1) % 2)

            pe.wait_ge(post_in, 16 * N_POST)
            pe.wait_ge(o_evac, B)
            pe.wait_ge(exp_done, B * NC)
            for u in range(NQ * ST):
                q, g = divmod(u, ST)
                wait(pe, rec_done, u - 3)
                pe.matmul(sc_ps[:, u % 4, 0:QW], sumsel[:, :], ctxo[:, g, q * QW:(q + 1) * QW],
                          start=True, stop=True).then_inc(sum_done, 1)
            for t in range(NT):
                pe.wait_ge(norm_done, ST * (-(-(t + 1) * P // QW)))
                wait(pe, dlt_evac, t - 3)
                for g in range(ST):
                    last = pe.matmul(spare_ps[t % 4][:, 0:D], ctxo[:, g, t * P:(t + 1) * P], wo[:, g, :],
                                     start=(g == 0), stop=(g == ST - 1))
                last.then_inc(op_done, 1)
            pe.wait_ge(rec_done, NQ * ST)
            pe.wait_ge(wr_split, 2)

            def router(t):
                pe.wait_ge(ylo_done, t + 1)
                ts = slice(t * P, (t + 1) * P)
                for k in range(KD):
                    last = mm3(o_ps[:, t * NE:(t + 1) * NE], yT_hi[:, k, ts], yT_lo[:, k, ts], wr_hi[:, k, :], wr_lo[:, k, :],
                               k == 0, k == KD - 1)
                last.then_inc(lg_done, 1)

            pe.wait_ge(dlt_evac, NT)
            for t in range(NT):
                pe.wait_ge(y_done, t + 1)
                wait(pe, ylo_done, t - 3)
                for k in range(KD):
                    last = pe.transpose(sc_ps[:, t % 4, k * P:(k + 1) * P], dlt[:, t, k * P:(k + 1) * P], ident[:, :])
                last.then_inc(yt_done, 1)
                if t > 0:
                    router(t - 1)
            router(NT - 1)

            def fc(f, e):
                u = f * NE + e
                wait(pe, relu_done, u - 1)
                for m in range(KD):
                    ws = slice(m * P, (m + 1) * P)
                    for k in range(KD):
                        last = mm3(sc_ps[:, e % 2, m * FT:(m + 1) * FT], wf_hi[:, e, k, ws], wf_lo[:, e, k, ws],
                                   yT_hi[:, k, bass.ds(f * FT, FT)], yT_lo[:, k, bass.ds(f * FT, FT)], k == 0, k == KD - 1)
                last.then_inc(fc_done, 1)

            def proj(f, e):
                u = f * NE + e
                pe.wait_ge(hlo_done, u + 1)
                wait(pe, acc_done, 2 * u - 2)
                for t in range(2):
                    ts = slice(t * P, (t + 1) * P)
                    for k in range(KD):
                        last = mm3(sc_ps[:, 2 + e % 2, t * D:(t + 1) * D], h_hi[:, e % NB, k, ts], h_lo[:, e % NB, k, ts],
                                   wp_hi[:, e, k, :], wp_lo[:, e, k, :], k == 0, k == KD - 1)
                last.then_inc(y2_done, 1)

            def experts(f, first=False):
                for e in range(NE):
                    if first:
                        pe.wait_ge(we_lo, 2 * (e + 1))
                    fc(f, e)
                    if e >= 2:
                        proj(f, e - 2)
                    elif not first:
                        proj(f - 1, NE - 2 + e)

            experts(0, first=True)
            with pe.Fori(1, NF) as f:
                experts(f)
            proj(NF - 1, NE - 2)
            proj(NF - 1, NE - 1)

        @block.scalar
        def _(act):
            def k_hi_evac(n, m, s):
                act.wait_ge(kproj_done, KD * n + m + 1)
                wait(act, scores_done, GC * (n - 1))
                for half in range(2):
                    rows = slice(half * 64, half * 64 + 64)
                    act.activation(kst[rows, s, 2 * m + half, :], k_ps[rows, m, 0:TG], ACT.Identity,
                                   bias=bk[rows, m:m + 1]).then_inc(k_hi, 1)

            def exps(b, j):
                n = b * NC + j
                act.wait_ge(scores_done, n + 1)
                wait(act, pv_done, n - 2)
                act.activation(prob[0:TC, j % 3, :].rearrange("p (c n) -> p c n", c=2),
                               sc_ps[0:TC, 2 * (j % 2):2 * (j % 2) + 2, 0:NH * S // 2], ACT.Exp,
                               scale=m_scale[0:TC, bass.ds(n, 1)], bias=m_bias[0:TC, bass.ds(n, 1)]).then_inc(exp_done, 1)

            def batch(b, par, final=False):
                for j in range(NC):
                    g = j // GC
                    exps(b, j)
                    if j % GC < KD and not (final and g == NG - 1):
                        k_hi_evac(b * NG + g + 1, j % GC, (par + g + 1) % 2)

            act.wait_ge(var_done, 1)
            act.activation(std[:, :], var_e[:, :], ACT.Sqrt).then_inc(std_done, 1)
            for t in range(NT):
                act.wait_ge(xt_done, t + 1)
                act.activation(xnT[:, :, t * P:(t + 1) * P], sc_ps[:, t % 4, 0:D].rearrange("p (k n) -> p k n", k=KD),
                               ACT.Copy).then_inc(xT_done, 1)
            act.wait_ge(w_in, 16 * N_W)
            for m in range(KD):
                k_hi_evac(0, m, 0)
            for u in range(NQ * ST):
                q, i = divmod(u, ST)
                act.wait_ge(qp_done, u + 1)
                act.activation(qT[:, i, q * QW:(q + 1) * QW], sc_ps[:, u % 4, 0:QW], ACT.Identity,
                               bias=bq2[:, i:i + 1]).then_inc(qT_done, 1)
            act.activation(tg[:, :], gates[:, 0:2], ACT.Tanh).then_inc(tanh_done, 1)
            act.wait_ge(m_ready, 2)
            batch(0, 0)
            batch(1, 1)
            with act.Fori(1, B // 2 - 1) as i:
                batch(2 * i, 0)
                batch(2 * i + 1, 1)
            batch(B - 2, 0)
            batch(B - 1, 1, final=True)

            for n in range(2):
                act.wait_ge(var_done, n + 2)
                act.activation(std[:, :], var_e[:, :], ACT.Sqrt).then_inc(std_done, 1)
            for e in range(NE):
                act.wait_ge(wraw_in[e % 2], 32 * (e // 2 + 1))
                for i, dst in enumerate((wf_hi, wp_hi)):
                    act.activation(dst[:, e, :, :], w_raw[:, e % 2, i, :, :], ACT.Copy).then_inc(we_hi, 1)
            for t in range(NT):
                act.wait_ge(yt_done, t + 1)
                act.activation(yT_hi[:, :, t * P:(t + 1) * P], sc_ps[:, t % 4, 0:D].rearrange("p (k n) -> p k n", k=KD),
                               ACT.Copy).then_inc(yhi_done, 1)
            act.wait_ge(diff_done, 1)
            act.activation(e21[:, :], e21[:, :], ACT.Exp).then_inc(e21_done, 1)

            def hidden(f, first=False):
                for e in range(NE):
                    u = f * NE + e
                    act.wait_ge(fc_done, u + 1)
                    if not (first and e < 2):
                        act.wait_ge(sq_done, u - 1)
                    act.activation(h_relu[:, e % 2, :, :], sc_ps[:, e % 2, :].rearrange("p (m n) -> p m n", m=KD),
                                   ACT.Relu).then_inc(relu_done, 1)
                    act.wait_ge(sq_done, u + 1)
                    if not (first and e < NB):
                        act.wait_ge(y2_done, u - NB + 1)
                    act.activation(h_hi[:, e % NB, :, :], h_sq[:, e % 2, :, :], ACT.Copy).then_inc(hhi_done, 1)

            hidden(0, first=True)
            with act.Fori(1, NF) as f:
                hidden(f)

        @block.vector
        def _(dve):
            seq = [0]

            def then(ins):
                seq[0] += 1
                ins.then_inc(dve_seq, 1)
                dve.wait_ge(dve_seq, seq[0])

            def stats(done, src):
                for t in range(NT):
                    done(t)
                    last = dve.bn_stats(st6[:, t, :], src[:, t, :])
                then(last)
                for t in range(NT):
                    last = dve.bn_aggr(mv[:, t, :], st6[:, t, :])
                then(last)
                dve.tensor_scalar(var_e[:, :], mv[:, :, 1], EPS, None, ALU.add).then_inc(var_done, 1)

            def inv_std(n):
                dve.wait_ge(std_done, n)
                then(dve.reciprocal(rstd[:, :], std[:, :]))

            def k_lo_evac(n, m, s):
                for half in range(2):
                    dve.wait_ge(k_hi, 2 * KD * n + 2 * m + half + 1)
                    rows, other = slice(half * 64, half * 64 + 64), slice(64 - half * 64, 128 - half * 64)
                    dve.scalar_tensor_tensor(kst[other, s, 2 * m + half, :], k_ps[rows, m, 0:TG], bk[rows, m:m + 1],
                                             plain(kst[rows, s, 2 * m + half, :]), ALU.add, ALU.subtract).then_inc(k_lo, 1)

            def v_evac_step(n, j, s):
                dve.wait_ge(vproj_done, n * GC + j + 1)
                wait(dve, pv_done, (n - 1) * GC)
                dve.tensor_tensor(vst[0:TC, s, j, :, 0:HD], v_ps[0:TC, 0:D].rearrange("p (h d) -> p h d", h=NH),
                                  bv[0:TC, :].rearrange("p (h d) -> p h d", h=NH), ALU.add).then_inc(v_evac, 1)

            def q_expand(b, par):
                src = qT[:, :, bass.ds(b * S, S)]
                wait(dve, q_ready, 2 * b)
                dve.tensor_copy(q_rnd[:, :, :], src).then_inc(q_step, 1)
                dve.wait_ge(q_step, 2 * b + 1)
                dve.tensor_tensor(q_rem[:, :, :], src, plain(q_rnd[:, :, :]), ALU.subtract).then_inc(q_step, 1)
                dve.wait_ge(q_step, 2 * b + 2)
                wait(dve, scores_done, NC * (b - 1))
                heads = hmask[:, :].unsqueeze(1).unsqueeze(3).to_broadcast([P, ST, HS, S])
                for dst, part in ((q_hi, plain(q_rnd[:, :, :])), (q_lo, q_rem[:, :, :])):
                    dve.tensor_tensor(dst[:, par, :, :, :], part.unsqueeze(2).to_broadcast([P, ST, HS, S]), heads,
                                      ALU.mult).then_inc(q_ready, 1)

            def o_evac_step(b):
                dve.wait_ge(pv_done, NC * (b + 1))
                dve.tensor_copy(ctxo[:, :, bass.ds(b * S, S)],
                                o_ps[:, 0:ST * S].rearrange("p (c n) -> p c n", c=ST)).then_inc(o_evac, 1)

            def batch(b, par, first=False, final=False):
                for j in range(NC):
                    n, g = b * NC + j, j // GC
                    dve.wait_ge(exp_done, n + 1)
                    p = prob[0:TC, j % 3, :]
                    dve.tensor_scalar(p, p, EXP_LO, EXP_HI, ALU.max, ALU.min).then_inc(clip_done, 1)
                    if not (final and g == NG - 1):
                        if j % GC < KD:
                            k_lo_evac(b * NG + g + 1, j % GC, (par + g + 1) % 2)
                        v_evac_step(b * NG + g + 1, j % GC, (par + g + 1) % 2)
                    if j == 0 and not first:
                        o_evac_step(b - 1)
                    if j == NC // 2 and not final:
                        q_expand(b + 1, 1 - par)

            dve.wait_ge(w_in, 16 * N_W)
            for src, dst in ((wk, wk_hi), (wv, wv_hi)):
                dve.tensor_copy(dst[:, :, :], src[:, :, :]).then_inc(w_split, 1)
            dve.wait_ge(w_split, 2)
            for src, hi, lo in ((wk, wk_hi, wk_lo), (wv, wv_hi, wv_lo)):
                dve.tensor_tensor(lo[:, :, :], src[:, :, :], plain(hi[:, :, :]), ALU.subtract).then_inc(w_split, 1)
            dve.wait_ge(x_in, 16 * N_X)
            stats(lambda t: None, x_sb)
            for r in range(2):
                dve.tensor_copy(wq2[:, :, :, r, :], wq[:, :, :].rearrange("p k (i c) -> p k i c", i=ST)).then_inc(w_split, 1)
            inv_std(1)
            for t in range(NT):
                wait(dve, xt_done, t - 1)
                dve.tensor_scalar(xn[:, t % 2, :], x_sb[:, t, :], mv[:, t, 0:1], rstd[:, t:t + 1],
                                  ALU.subtract, ALU.mult).then_inc(xn_done, 1)
            dve.tensor_scalar(m_scale[0:TC, :], mask_i[0:TC, :], 0.5, SCALE, ALU.is_gt, ALU.mult).then_inc(m_ready, 1)
            dve.wait_ge(m_ready, 1)
            dve.tensor_scalar(m_bias[0:TC, :], m_scale[0:TC, :], CLIP / SCALE, -CLIP, ALU.mult, ALU.add).then_inc(m_ready, 1)
            for m in range(KD):
                k_lo_evac(0, m, 0)
            dve.wait_ge(v_ones, 1)
            for j in range(GC):
                v_evac_step(0, j, 0)
            dve.wait_ge(qT_done, NQ * ST)
            q_expand(0, 0)
            batch(0, 0, first=True)
            batch(1, 1)
            with dve.Fori(1, B // 2 - 1) as i:
                batch(2 * i, 0)
                batch(2 * i + 1, 1)
            batch(B - 2, 0)
            batch(B - 1, 1, final=True)
            o_evac_step(B - 1)

            dve.wait_ge(post_in, 16 * N_POST)
            dve.wait_ge(tanh_done, 1)
            then(dve.tensor_scalar(rs[:, :], gates[:, 2:3], 0.0, RES_SCALE_MAX, ALU.max, ALU.min))
            dve.tensor_scalar(bo[:, :], bo[:, :], rs[:, 0:1], None, ALU.mult)
            then(dve.tensor_scalar(gam[:, :], gam[:, :], tg[:, 0:1], None, ALU.mult))
            for u in range(NQ * ST):
                dve.wait_ge(sum_done, u + 1)
                wait(dve, norm_done, u - 1)
                dve.reciprocal(rec[:, u % 2, :], sc_ps[:, u % 4, 0:QW]).then_inc(rec_done, 1)

            def delta(t):
                dve.wait_ge(op_done, t + 1)
                dve.scalar_tensor_tensor(dlt[:, t, :], spare_ps[t % 4][:, 0:D], rs[:, 0:1], bo[:, :],
                                         ALU.mult, ALU.add).then_inc(dlt_evac, 1)
                dve.wait_ge(dlt_evac, t + 1)

            stats(delta, dlt)
            for src, hi, lo in ((wr, wr_hi, wr_lo),):
                dve.tensor_copy(hi[:, :, :], src[:, :, :]).then_inc(wr_split, 1)
                dve.wait_ge(wr_split, 1)
                dve.tensor_tensor(lo[:, :, :], src[:, :, :], plain(hi[:, :, :]), ALU.subtract).then_inc(wr_split, 1)
            inv_std(2)
            for t in range(NT):
                dve.tensor_scalar(dlt[:, t, :], dlt[:, t, :], mv[:, t, 0:1], rstd[:, t:t + 1],
                                  ALU.subtract, ALU.mult).then_inc(dlt_done, 1)
            dve.wait_ge(dlt_done, NT)
            stats(lambda t: dve.wait_ge(x1_done, t + 1), x_sb)
            inv_std(3)
            for t in range(NT):
                dve.tensor_scalar(dlt[:, t, :], x_sb[:, t, :], mv[:, t, 0:1], rstd[:, t:t + 1],
                                  ALU.subtract, ALU.mult).then_inc(y_done, 1)
            for e in range(NE):
                for i, (hi, lo) in enumerate(((wf_hi, wf_lo), (wp_hi, wp_lo))):
                    dve.wait_ge(we_hi, 2 * e + i + 1)
                    dve.tensor_tensor(lo[:, e, :, :], w_raw[:, e % 2, i, :, :], plain(hi[:, e, :, :]),
                                      ALU.subtract).then_inc(we_lo, 1)
            for t in range(NT):
                dve.wait_ge(yhi_done, t + 1)
                ts = slice(t * P, (t + 1) * P)
                dve.tensor_tensor(yT_lo[:, :, ts], sc_ps[:, t % 4, 0:D].rearrange("p (k n) -> p k n", k=KD),
                                  plain(yT_hi[:, :, ts]), ALU.subtract).then_inc(ylo_done, 1)
            per_tile = [P, NT, NE]
            revs = rev_e[:, :].unsqueeze(1).to_broadcast(per_tile)

            def over_e(ap):
                return ap.unsqueeze(2).to_broadcast(per_tile)

            def largest(top, pick):
                then(dve.tensor_reduce(top[:, :], logit[:, :, :], AX.X, ALU.max))
                then(dve.tensor_tensor(hit[:, :, :], logit[:, :, :], over_e(top[:, :]), ALU.is_equal))
                then(dve.tensor_tensor(hit[:, :, :], hit[:, :, :], revs, ALU.mult))
                then(dve.tensor_reduce(firstof[:, :], hit[:, :, :], AX.X, ALU.max))
                then(dve.tensor_tensor(pick[:, :, :], revs, over_e(firstof[:, :]), ALU.is_equal))

            dve.wait_ge(lg_done, NT)
            then(dve.tensor_copy(logit[:, :, :], o_ps[:, 0:NT * NE].rearrange("p (t e) -> p t e", t=NT)))
            largest(top1, pick1)
            then(dve.scalar_tensor_tensor(logit[:, :, :], pick1[:, :, :], -BIG, logit[:, :, :], ALU.mult, ALU.add))
            largest(top2, pick2)
            dve.tensor_tensor(e21[:, :], top2[:, :], top1[:, :], ALU.subtract).then_inc(diff_done, 1)
            dve.wait_ge(e21_done, 1)
            then(dve.tensor_scalar(pr2[:, :], e21[:, :], 1.0, None, ALU.add))
            then(dve.reciprocal(pr1[:, :], pr2[:, :]))
            then(dve.tensor_scalar(pr1[:, :], pr1[:, :], tg[:, 1:2], None, ALU.mult))
            then(dve.tensor_tensor(pr2[:, :], pr1[:, :], e21[:, :], ALU.mult))
            dve.tensor_tensor(pick1[:, :, :], pick1[:, :, :], over_e(pr1[:, :]), ALU.mult)
            then(dve.tensor_tensor(pick2[:, :, :], pick2[:, :, :], over_e(pr2[:, :]), ALU.mult))
            then(dve.tensor_tensor(w_tok[:, :, :], pick1[:, :, :], pick2[:, :, :], ALU.add))

            def accumulate(f, e):
                u = f * NE + e
                dve.wait_ge(y2_done, u + 1)
                for t in range(2):
                    tile = f * 2 + t
                    if e > 0:
                        dve.wait_ge(acc_done, 2 * u - 1 + t)
                    acc = x_sb[:, bass.ds(tile, 1), :].squeeze(1)
                    dve.scalar_tensor_tensor(acc, sc_ps[:, 2 + e % 2, t * D:(t + 1) * D],
                                             w_tok[:, bass.ds(tile, 1), e], acc, ALU.mult, ALU.add).then_inc(acc_done, 1)

            def experts(f, first=False):
                for e in range(NE):
                    u = f * NE + e
                    dve.wait_ge(relu_done, u + 1)
                    if not (first and e < 2):
                        dve.wait_ge(hlo_done, u - 1)
                    r = h_relu[:, e % 2, :, :]
                    dve.tensor_tensor(h_sq[:, e % 2, :, :], r, r, ALU.mult).then_inc(sq_done, 1)
                    if e >= 2:
                        accumulate(f, e - 2)
                    elif not first:
                        accumulate(f - 1, NE - 2 + e)

            experts(0, first=True)
            with dve.Fori(1, NF) as f:
                experts(f)
            accumulate(NF - 1, NE - 2)
            accumulate(NF - 1, NE - 1)


def kernel(x, ctx_2048, mask_BxS2_ik0, g_xattn, g_ffn, L0_xattn_Wq, L0_xattn_bq, L0_xattn_Wk, L0_xattn_bk,
           L0_xattn_Wv, L0_xattn_bv, L0_xattn_Wo, L0_xattn_bo, L0_xattn_ln_gamma, L0_xattn_ln_beta,
           L0_xattn_residual_scale, L0_ffn_w_router, L0_ffn_w_fc, L0_ffn_w_proj):
    import numpy as np
    import concourse.bacc as bacc
    from concourse.bass_utils import run_bass_kernel_spmd

    def rows(w):
        w = np.asarray(w)
        w = w.reshape(w.shape[:-2] + (KD, P, w.shape[-1]))
        return np.ascontiguousarray(np.moveaxis(w, -3, -2))

    def row(v):
        return np.ascontiguousarray(np.asarray(v).reshape(1, -1))

    ctxT = np.asarray(ctx_2048).reshape(B, NG, TG, KD, P).transpose(0, 1, 4, 3, 2)
    wo = np.zeros((ST, 32, ST, D), np.float32)
    wo[:, 0:HD] = np.asarray(L0_xattn_Wo).T.reshape(ST, ST, HD, D).transpose(1, 2, 0, 3)
    r = np.arange(P)
    arrays = {
        "x": np.ascontiguousarray(np.asarray(x).reshape(NT, P, D).transpose(1, 0, 2)),
        "ctxT": np.ascontiguousarray(ctxT),
        "mask": np.ascontiguousarray(np.asarray(mask_BxS2_ik0).reshape(B * NC, TC).T),
        "wk": rows(np.asarray(L0_xattn_Wk).T), "wv": rows(np.asarray(L0_xattn_Wv).T), "wq": rows(np.asarray(L0_xattn_Wq).T),
        "wo": wo.reshape(P, ST, D), "wr": rows(L0_ffn_w_router), "wf": rows(L0_ffn_w_fc), "wp": rows(L0_ffn_w_proj),
        "bk": np.ascontiguousarray(np.asarray(L0_xattn_bk).reshape(KD, P).T),
        "bq2": np.ascontiguousarray(np.tile(np.asarray(L0_xattn_bq).reshape(ST, HW).T, (2, 1))),
        "bv": row(L0_xattn_bv), "bo": row(L0_xattn_bo), "gamma": row(L0_xattn_ln_gamma), "beta": row(L0_xattn_ln_beta),
        "g_xattn": row(g_xattn), "g_ffn": row(g_ffn), "rscale": row(L0_xattn_residual_scale),
        "ident": np.eye(P, dtype=np.float32),
        "sumsel": (r[:, None] == r[None, :] // 32 * 32 + HD).astype(np.float32),
        "hmask": (r[:, None] % HW // HD == np.arange(HS)[None, :]).astype(np.float32),
        "rev_e": np.tile(NE - np.arange(NE, dtype=np.float32), (P, 1)),
    }
    nc = bacc.Bacc("TRN2", target_bir_lowering=False, num_devices=1)
    args = {k: nc.dram_tensor(f"in_{k}", v.shape, mybir.dt.from_np(v.dtype), kind="ExternalInput").ap()
            for k, v in arrays.items()}
    out = nc.dram_tensor("out_y", (P, NT, D), mybir.dt.float32, kind="ExternalOutput").ap()
    gated_cross_attention_moe(nc, args, out)
    got = run_bass_kernel_spmd(nc, [{f"in_{k}": v for k, v in arrays.items()}], core_ids=[0])
    y = got.results[0]["out_y"]
    return np.ascontiguousarray(y.transpose(1, 0, 2)).reshape(B, S, D)
```

```python
import concourse.bass as bass
from concourse import mybir
from contextlib import ExitStack

B, S, D, T = 32, 56, 256, 1500
NH, HD = 16, 16
P = 128
KD = D // P
TC = 125
GC = 4
TG = TC * GC
NG = T // TG
NC = NG * GC
TOK = B * S
NT = TOK // P
NP = B // 2
PW = 2 * S
PG = 2 * NG
PC = 2 * NC
RT = 12
ST = 4
HS = NH // ST
HW = HS * HD
NE = 8
FT = 256
NF = TOK // FT
VW = HD + 1
PB = 4
NW = 2 * NE
NB = 4
EPS = 1e-5
CLIP = 50.0
EXP_HI = 5.184705528587072e21
EXP_LO = 1.9287498479639178e-22
BIG = 3.0e38
SCALE = HD ** -0.5
RES_SCALE_MAX = 0.3


def gated_cross_attention_moe(nc, a, x1_dram, out):
    fp32, fp32r, i32 = mybir.dt.float32, mybir.dt.float32r, mybir.dt.int32
    ALU = mybir.AluOpType
    ACT = mybir.ActivationFunctionType
    AX = mybir.AxisListType

    with ExitStack() as ctx:
        def sem(name):
            return ctx.enter_context(nc.semaphore(name))

        def sb(name, shape, dt=fp32, scope=ctx):
            return scope.enter_context(nc.sbuf_tensor(name, shape, dt))

        def plain(ap):
            return ap.bitcast(fp32)

        def wait(eng, s, value):
            if not isinstance(value, int) or value > 0:
                eng.wait_ge(s, value)

        yT_hi = sb("yT_hi", [P, KD, TOK], fp32r)
        yT_lo = sb("yT_lo", [P, KD, TOK], fp32r)
        we_hi = sb("we_hi", [P, NW, KD, D], fp32r)
        we_lo = sb("we_lo", [P, NW, KD, D], fp32r)
        w_raw = sb("w_raw", [P, KD, D])
        wo = sb("wo", [P, ST, D])
        wr = sb("wr", [P, KD, NE])
        wr_hi = sb("wr_hi", [P, KD, NE], fp32r)
        wr_lo = sb("wr_lo", [P, KD, NE], fp32r)
        bo = sb("bo", [P, D])
        gam = sb("gam", [P, D])
        bet = sb("bet", [P, D])
        ident = sb("ident", [P, P])
        sumsel = sb("sumsel", [P, P])
        gates = sb("gates", [P, 3])
        tg = sb("tg", [P, 2])
        rs = sb("rs", [P, 1])
        rev_e = sb("rev_e", [P, NE])
        held = [sb(f"held_{i}", [P, 1]) for i in range(3)]
        xq = sb("xq", [P, D])
        xn = sb("xn", [P, D])
        xr = sb("xr", [P, D])
        dlt = sb("dlt", [P, D])
        x1 = sb("x1", [P, D])
        ctxo = sb("ctxo", [P, ST, PW])
        rec = sb("rec", [P, ST, PW])
        mhalf = sb("mhalf", [P, 1])
        st6 = [sb(f"st6_{i}", [P, 6]) for i in range(3)]
        mv = [sb(f"mv_{i}", [P, 2]) for i in range(3)]
        var_e = [sb(f"var_e_{i}", [P, 1]) for i in range(3)]
        rstd = [sb(f"rstd_{i}", [P, 1]) for i in range(3)]

        att = ExitStack()
        wk_hi = sb("wk_hi", [P, KD, D], fp32r, scope=att)
        wk_lo = sb("wk_lo", [P, KD, D], fp32r, scope=att)
        wv_hi = sb("wv_hi", [P, KD, D], fp32r, scope=att)
        wv_lo = sb("wv_lo", [P, KD, D], fp32r, scope=att)
        wq = sb("wq", [P, KD, D], scope=att)
        bq = sb("bq", [P, KD], scope=att)
        bk = sb("bk", [P, KD], scope=att)
        bv = sb("bv", [P, D], scope=att)
        hmask = sb("hmask", [P, HS], scope=att)
        m_scale = sb("m_scale", [P, B * NC], scope=att)
        m_bias = sb("m_bias", [P, B * NC], scope=att)
        one = sb("one", [P, KD], scope=att)
        xnT = sb("xnT", [P, KD, PW], scope=att)
        qT = sb("qT", [P, ST, PW], scope=att)
        raw = sb("raw", [P, 2, KD, TG], scope=att)
        c_hi = sb("c_hi", [P, 2, KD, TG], fp32r, scope=att)
        c_lo = sb("c_lo", [P, 2, KD, TG], fp32r, scope=att)
        kst = sb("kst", [P, 2, ST, TG], fp32r, scope=att)
        vst = sb("vst", [P, 2, GC, NH, VW], scope=att)
        q_rnd = sb("q_rnd", [P, ST, S], fp32r, scope=att)
        q_rem = sb("q_rem", [P, ST, S], scope=att)
        q_hi = sb("q_hi", [P, 2, ST, HS, S], fp32r, scope=att)
        q_lo = sb("q_lo", [P, 2, ST, HS, S], fp32r, scope=att)
        early = ExitStack()
        wk = sb("wk", [P, KD, D], scope=early)
        wv = sb("wv", [P, KD, D], scope=early)
        mask_i = sb("mask_i", [P, B * NC], i32, scope=early)
        early.close()
        prob = sb("prob", [P, PB, NH * S], scope=att)
        att.close()

        ffn = ExitStack()
        acc = sb("acc", [P, NT, D], scope=ffn)
        h_relu = sb("h_relu", [P, 2, KD, FT], scope=ffn)
        h_sq = sb("h_sq", [P, 2, KD, FT], scope=ffn)
        h_hi = sb("h_hi", [P, NB, KD, FT], fp32r, scope=ffn)
        h_lo = sb("h_lo", [P, NB, KD, FT], fp32r, scope=ffn)
        logit = sb("logit", [P, NT, NE], scope=ffn)
        hit = sb("hit", [P, NT, NE], scope=ffn)
        pick1 = sb("pick1", [P, NT, NE], scope=ffn)
        pick2 = sb("pick2", [P, NT, NE], scope=ffn)
        w_tok = sb("w_tok", [P, NT, NE], scope=ffn)
        top1 = sb("top1", [P, NT], scope=ffn)
        top2 = sb("top2", [P, NT], scope=ffn)
        firstof = sb("firstof", [P, NT], scope=ffn)
        e21 = sb("e21", [P, NT], scope=ffn)
        pr1 = sb("pr1", [P, NT], scope=ffn)
        pr2 = sb("pr2", [P, NT], scope=ffn)
        ffn.close()

        sc_ps = ctx.enter_context(nc.psum_tensor("sc_ps", [P, 4, 512], fp32))
        k_ps = ctx.enter_context(nc.psum_tensor("k_ps", [P, KD, 512], fp32))
        v_ps = ctx.enter_context(nc.psum_tensor("v_ps", [P, 512], fp32))
        o_ps = ctx.enter_context(nc.psum_tensor("o_ps", [P, 512], fp32))
        side_ps = k_ps[:, 0, :]
        logit_ps = [k_ps[:, 1, :], o_ps[:, :]]

        w_in = sem("w_in")
        t_in = sem("t_in")
        ones_done = sem("ones_done")
        o_clear = sem("o_clear")
        w_split = sem("w_split")
        m_ready = sem("m_ready")
        tanh_done = sem("tanh_done")
        scale_done = sem("scale_done")
        wr_split = sem("wr_split")
        raw_in = [sem(f"raw_in{i}") for i in range(2)]
        ctx_hi = sem("ctx_hi")
        ctx_split = sem("ctx_split")
        kproj_done = sem("kproj_done")
        vproj_done = sem("vproj_done")
        k_hi = sem("k_hi")
        k_lo = sem("k_lo")
        v_evac = sem("v_evac")
        q_step = sem("q_step")
        q_ready = sem("q_ready")
        scores_done = sem("scores_done")
        exp_done = sem("exp_done")
        clip_done = sem("clip_done")
        pv_done = sem("pv_done")
        o_evac = sem("o_evac")
        xq_in = sem("xq_in")
        xn_done = sem("xn_done")
        xt_done = sem("xt_done")
        xT_done = sem("xT_done")
        qp_done = sem("qp_done")
        qT_done = sem("qT_done")
        xr_in = sem("xr_in")
        xb_done = sem("xb_done")
        sum_done = sem("sum_done")
        sum_evac = sem("sum_evac")
        rec_done = sem("rec_done")
        norm_done = sem("norm_done")
        op_done = sem("op_done")
        dlt_evac = sem("dlt_evac")
        x1_step = sem("x1_step")
        x1_done = sem("x1_done")
        x1_out = sem("x1_out")
        y_done = sem("y_done")
        yt_done = sem("yt_done")
        yhi_done = sem("yhi_done")
        ylo_done = sem("ylo_done")
        ln_step = [sem(f"ln_step{i}") for i in range(3)]
        var_done = [sem(f"var_done{i}") for i in range(3)]
        rstd_done = [sem(f"rstd_done{i}") for i in range(3)]
        wraw_in = sem("wraw_in")
        wehi_done = sem("wehi_done")
        welo_done = sem("welo_done")
        lg_done = sem("lg_done")
        diff_done = sem("diff_done")
        e21_done = sem("e21_done")
        acc_in = [sem(f"acc_in{i}") for i in range(2)]
        fc_done = sem("fc_done")
        relu_done = sem("relu_done")
        sq_done = sem("sq_done")
        hhi_done = sem("hhi_done")
        hlo_done = sem("hlo_done")
        y2_done = sem("y2_done")
        acc_done = sem("acc_done")
        out_done = sem("out_done")
        dve_seq = sem("dve_seq")

        N_W, N_T = 8, 10

        block = ctx.enter_context(nc.Block())

        def bcast(ap, n):
            return ap.partition_broadcast(n)

        @block.sync
        def _(sp):
            sp.dma_start(xq[0:PW, :], a["x"][0:PW, :]).then_inc(xq_in, 16)
            sp.dma_start(raw[:, 0, :, :], a["ctxT"][0]).then_inc(raw_in[0], 16)
            for dst, src in ((wk, "wk"), (wv, "wv"), (wq, "wq")):
                sp.dma_start(dst[:, :, :], a[src]).then_inc(w_in, 16)
            sp.dma_start(bk[:, :], a["bk"]).then_inc(w_in, 16)
            sp.dma_start(bq[:, :], a["bq"]).then_inc(w_in, 16)
            sp.dma_start(bv[:, :], bcast(a["bv"], P)).then_inc(w_in, 16)
            sp.dma_start(hmask[:, :], a["hmask"]).then_inc(w_in, 16)
            sp.dma_start(mask_i[0:TC, :], a["mask"]).then_inc(w_in, 16)
            sp.dma_start(raw[:, 1, :, :], a["ctxT"][1]).then_inc(raw_in[1], 16)

            def load_group(n, s):
                wait(sp, ctx_split, n - 1)
                sp.dma_start(raw[:, s, :, :], a["ctxT"][bass.ds(n, 1)].squeeze(0)).then_inc(raw_in[s], 16)

            for n in range(2, PG):
                load_group(n, n % 2)
            with sp.Fori(1, NP) as i:
                for q in range(PG):
                    load_group(i * PG + q, q % 2)
            sp.wait_ge(pv_done, B * NC)
            for part, (t0, t1, pairs) in enumerate(((0, RT, NP - 1), (RT, NT, NP))):
                sp.wait_ge(x1_out, 16 * pairs)
                sp.dma_start(acc[:, t0:t1, :], x1_dram[t0 * P:t1 * P, :].rearrange("(t p) d -> p t d", p=P))\
                    .then_inc(acc_in[part], 16)
            for f in range(NF):
                sp.wait_ge(acc_done, 2 * NE * (f + 1))
                sp.dma_start(out[:, 2 * f:2 * f + 2, :], acc[:, 2 * f:2 * f + 2, :]).then_inc(out_done, 16)
            sp.wait_ge(out_done, 16 * NF)

        @block.gpsimd
        def _(pool):
            pool.memset(one[:, :], 1.0).then_inc(ones_done, 1)
            pool.memset(mhalf[:, :], -0.5).then_inc(ones_done, 1)
            pool.memset(vst[:, :, :, :, HD:VW], 1.0).then_inc(ones_done, 1)
            pool.wait_ge(ones_done, 3)

            def split(n, s, count):
                pool.wait_ge(raw_in[s], 16 * count)
                wait(pool, vproj_done, GC * (n - 1))
                r = raw[:, s, :, :]
                pool.tensor_tensor(c_hi[:, s, :, :], r, one[:, :].unsqueeze(2).to_broadcast([P, KD, TG]),
                                   ALU.mult).then_inc(ctx_hi, 1)
                pool.wait_ge(ctx_hi, n + 1)
                pool.tensor_tensor(c_lo[:, s, :, :], r, plain(c_hi[:, s, :, :]), ALU.subtract).then_inc(ctx_split, 1)

            def inv_std(ln, i):
                pool.wait_ge(var_done[ln], i + 1)
                pool.tensor_tensor(rstd[ln][0:PW, :], var_e[ln][0:PW, :], mhalf[0:PW, :], ALU.pow)\
                    .then_inc(rstd_done[ln], 1)

            def x_plus_beta(i):
                pool.wait_ge(xr_in, 16 * i + 16)
                pool.tensor_tensor(xr[0:PW, :], xr[0:PW, :], bet[0:PW, :], ALU.add).then_inc(xb_done, 1)

            def expert_lo(i):
                pool.wait_ge(wehi_done, i + 1)
                pool.tensor_tensor(we_lo[:, bass.ds(i, 1), :, :].squeeze(1), w_raw[:, :, :],
                                   plain(we_hi[:, bass.ds(i, 1), :, :].squeeze(1)), ALU.subtract).then_inc(welo_done, 1)

            def pair(i, first=False, final=False):
                for q in range(2, PG + 2):
                    if not (final and q >= PG):
                        split(i * PG + q, q % 2, (i * PG + q) // 2 + 1 if isinstance(i, int) else i * NG + q // 2 + 1)
                    if q == 2 and not final:
                        inv_std(0, i + 1)
                        expert_lo(i)
                    if q == 2 and final:
                        expert_lo(i)
                    if q == 4 and not first:
                        x_plus_beta(i - 1)
                        inv_std(1, i - 1)
                    if q == 5 and not first:
                        inv_std(2, i - 1)

            split(0, 0, 1)
            inv_std(0, 0)
            split(1, 1, 1)
            pool.wait_ge(scale_done, 4)
            pair(0, first=True)
            with pool.Fori(1, NP - 1) as i:
                pair(i)
            pair(NP - 1, final=True)
            x_plus_beta(NP - 1)
            inv_std(1, NP - 1)
            inv_std(2, NP - 1)

            def h_low(f):
                for e in range(NE):
                    pool.wait_ge(hhi_done, f * NE + e + 1)
                    pool.tensor_tensor(h_lo[:, e % NB, :, :], h_sq[:, e % 2, :, :], plain(h_hi[:, e % NB, :, :]),
                                       ALU.subtract).then_inc(hlo_done, 1)

            with pool.Fori(0, NF) as f:
                h_low(f)

        @block.tensor
        def _(pe):
            def mm3(ps, w_h, w_l, m_h, m_l, first, last):
                pe.matmul(ps, w_h, m_h, start=first, stop=False)
                pe.matmul(ps, w_h, m_l, start=False, stop=False)
                return pe.matmul(ps, w_l, m_h, start=False, stop=last)

            def k_proj(n, m, s, side=None):
                if m == 0:
                    pe.wait_ge(ctx_split, n + 1)
                if side:
                    wait(pe, *side)
                wait(pe, k_lo, 4 * n - 4 + 2 * m + 2)
                ws = slice(m * P, (m + 1) * P)
                for k in range(KD):
                    last = mm3(k_ps[:, m, 0:TG], wk_hi[:, k, ws], wk_lo[:, k, ws], c_hi[:, s, k, :], c_lo[:, s, k, :],
                               k == 0, k == KD - 1)
                last.then_inc(kproj_done, 1)

            def v_proj(n, j, s):
                wait(pe, v_evac, n * GC + j)
                cs = slice(j * TC, (j + 1) * TC)
                for k in range(KD):
                    last = mm3(v_ps[0:TC, 0:D], c_hi[:, s, k, cs], c_lo[:, s, k, cs], wv_hi[:, k, :], wv_lo[:, k, :],
                               k == 0, k == KD - 1)
                last.then_inc(vproj_done, 1)

            def scores(i, c):
                n = i * PC + c
                b, g = c // NC, c // GC
                if c % NC == 0:
                    pe.wait_ge(q_ready, 4 * i + 2 * b + 2)
                if c % GC == 0:
                    pe.wait_ge(k_lo, 4 * (i * PG + g + 1))
                wait(pe, exp_done, n - 1)
                cs = slice(c % GC * TC, (c % GC + 1) * TC)
                for st in range(ST):
                    ps = sc_ps[0:TC, 2 * (c % 2) + st // 2, st % 2 * HS * S:(st % 2 + 1) * HS * S]
                    k = kst[:, g % 2, st, cs]
                    pe.matmul(ps, k, q_hi[:, b, st, :, :], start=True, stop=False)
                    last = pe.matmul(ps, k, q_lo[:, b, st, :, :], start=False, stop=True)
                last.then_inc(scores_done, 1)

            def pv(i, c):
                n = i * PC + c
                if c % NC == 0:
                    wait(pe, o_evac, 2 * i + c // NC)
                if c % 2 == 0:
                    pe.wait_ge(v_evac, n + 2)
                    pe.wait_ge(clip_done, n + 2)
                for h in range(NH):
                    col, q = divmod(h, ST)
                    last = pe.matmul(o_ps[q * 32:q * 32 + VW, col * S:(col + 1) * S], vst[0:TC, c // GC % 2, c % GC, h, :],
                                     prob[0:TC, c % PB, h * S:(h + 1) * S], start=(c % NC == 0 and col == 0),
                                     stop=(c % NC == NC - 1), skip_group_check=True)
                last.then_inc(pv_done, 1)

            def x_transpose(i):
                pe.wait_ge(xn_done, i + 1)
                for k in range(KD):
                    last = pe.transpose(side_ps[:, k * PW:(k + 1) * PW], xn[0:PW, k * P:(k + 1) * P], ident[0:PW, 0:PW])
                last.then_inc(xt_done, 1)

            def q_proj(i):
                pe.wait_ge(xT_done, i + 1)
                for m in range(KD):
                    for k in range(KD):
                        last = pe.matmul(side_ps[:, m * PW:(m + 1) * PW], wq[:, k, m * P:(m + 1) * P], xnT[:, k, :],
                                         start=(k == 0), stop=(k == KD - 1))
                last.then_inc(qp_done, 1)

            def spread_sums(i):
                pe.wait_ge(o_evac, 2 * i + 2)
                pe.matmul(side_ps[:, 0:ST * PW], sumsel[:, :], ctxo[:, :, :], start=True, stop=True).then_inc(sum_done, 1)

            def out_proj(i):
                pe.wait_ge(norm_done, i + 1)
                for col in range(ST):
                    last = pe.matmul(side_ps[0:PW, 0:D], ctxo[:, col, :], wo[:, col, :], start=(col == 0), stop=(col == ST - 1))
                last.then_inc(op_done, 1)

            def y_transpose(i):
                pe.wait_ge(y_done, i + 1)
                for k in range(KD):
                    last = pe.transpose(side_ps[:, k * PW:(k + 1) * PW], dlt[0:PW, k * P:(k + 1) * P], ident[0:PW, 0:PW])
                last.then_inc(yt_done, 1)

            def router(part, t):
                ts = slice(t * P, (t + 1) * P)
                for k in range(KD):
                    last = mm3(logit_ps[part][:, t * NE:(t + 1) * NE], yT_hi[:, k, ts], yT_lo[:, k, ts],
                               wr_hi[:, k, :], wr_lo[:, k, :], k == 0, k == KD - 1)
                last.then_inc(lg_done, 1)

            def pair(i, first=False, final=False):
                freed = {}
                if not first:
                    freed.update({0: (sum_evac, i), 2: (dlt_evac, i), 4: (ylo_done, i)})
                if not final:
                    freed.update({1: (xT_done, i + 2), 3: (qT_done, 4 * (i + 2))})
                for c in range(PC):
                    q, j = divmod(c, GC)
                    more = not (final and q == PG - 1)
                    scores(i, c)
                    if more and j < KD:
                        k_proj(i * PG + q + 1, j, (q + 1) % 2, freed.get(q - 1) if j == 0 else None)
                    if c % 2 == 0 and c > 0:
                        pv(i, c - 2)
                        pv(i, c - 1)
                    elif c == 0 and not first:
                        pv(i - 1, PC - 2)
                        pv(i - 1, PC - 1)
                    if more:
                        v_proj(i * PG + q + 1, j, (q + 1) % 2)
                    if j == 2:
                        if q < PG - 1:
                            pe.wait_ge(k_lo, 4 * (i * PG + q + 1) + 2)
                        if q == 0 and not first:
                            spread_sums(i - 1)
                        if q == 1 and not final:
                            x_transpose(i + 1)
                        if q == 2 and not first:
                            out_proj(i - 1)
                        if q == 3 and not final:
                            q_proj(i + 1)
                        if q == 4 and not first:
                            y_transpose(i - 1)
                    if not more:
                        if j == 0:
                            pe.wait_ge(ylo_done, NP - 1)
                            pe.wait_ge(wr_split, 2)
                            pe.wait_ge(k_lo, 4 * B * NG)
                        for t in range(j * RT // GC, (j + 1) * RT // GC):
                            router(0, t)

            pe.wait_ge(t_in, 16 * N_T)
            x_transpose(0)
            pe.wait_ge(w_split, 4)
            k_proj(0, 0, 0, (xT_done, 1))
            k_proj(0, 1, 0)
            for j in range(GC):
                v_proj(0, j, 0)
            pe.wait_ge(k_lo, 2)
            q_proj(0)
            pe.wait_ge(qT_done, 4)
            pe.wait_ge(o_clear, 1)
            pair(0, first=True)
            with pe.Fori(1, NP - 1) as i:
                pair(i)
            pair(NP - 1, final=True)
            pv(NP - 1, PC - 2)
            pv(NP - 1, PC - 1)
            spread_sums(NP - 1)
            out_proj(NP - 1)

            def fc(f, e):
                u = f * NE + e
                wait(pe, relu_done, u - 1)
                for m in range(KD):
                    ws = slice(m * P, (m + 1) * P)
                    for k in range(KD):
                        last = mm3(sc_ps[:, e % 2, m * FT:(m + 1) * FT], we_hi[:, 2 * e, k, ws], we_lo[:, 2 * e, k, ws],
                                   yT_hi[:, k, bass.ds(f * FT, FT)], yT_lo[:, k, bass.ds(f * FT, FT)], k == 0, k == KD - 1)
                last.then_inc(fc_done, 1)

            def proj(f, e):
                u = f * NE + e
                pe.wait_ge(hlo_done, u + 1)
                wait(pe, acc_done, 2 * u - 2)
                for t in range(2):
                    ts = slice(t * P, (t + 1) * P)
                    for k in range(KD):
                        last = mm3(sc_ps[:, 2 + e % 2, t * D:(t + 1) * D], h_hi[:, e % NB, k, ts], h_lo[:, e % NB, k, ts],
                                   we_hi[:, 2 * e + 1, k, :], we_lo[:, 2 * e + 1, k, :], k == 0, k == KD - 1)
                last.then_inc(y2_done, 1)

            def experts(f, first=False):
                for e in range(NE):
                    fc(f, e)
                    if e >= 2:
                        proj(f, e - 2)
                    elif not first:
                        proj(f - 1, NE - 2 + e)
                    if first and e == 3:
                        pe.wait_ge(dlt_evac, NP)
                        y_transpose(NP - 1)
                    if first and e == 6:
                        pe.wait_ge(ylo_done, NP)
                        for t in range(RT, NT):
                            router(1, t)

            pe.wait_ge(welo_done, NW)
            experts(0, first=True)
            with pe.Fori(1, NF) as f:
                experts(f)
            proj(NF - 1, NE - 2)
            proj(NF - 1, NE - 1)

        @block.scalar
        def _(act):
            def k_hi_evac(n, m, s):
                act.wait_ge(kproj_done, KD * n + m + 1)
                if m == 0:
                    wait(act, scores_done, GC * (n - 1))
                for half in range(2):
                    rows = slice(half * 64, half * 64 + 64)
                    act.activation(kst[rows, s, 2 * m + half, :], k_ps[rows, m, 0:TG], ACT.Identity,
                                   bias=bk[rows, m:m + 1]).then_inc(k_hi, 1)

            def exps(i, c):
                n = i * PC + c
                act.wait_ge(scores_done, n + 1)
                wait(act, pv_done, n - PB + 1)
                act.activation(prob[0:TC, c % PB, :].rearrange("p (c n) -> p c n", c=2),
                               sc_ps[0:TC, 2 * (c % 2):2 * (c % 2) + 2, 0:NH * S // 2], ACT.Exp,
                               scale=m_scale[0:TC, bass.ds(n, 1)], bias=m_bias[0:TC, bass.ds(n, 1)]).then_inc(exp_done, 1)

            def x_transposed(i):
                act.wait_ge(xt_done, i + 1)
                wait(act, qp_done, i)
                act.activation(xnT[:, :, :], side_ps[:, 0:KD * PW].rearrange("p (k n) -> p k n", k=KD),
                               ACT.Copy).then_inc(xT_done, 1)

            def sums_spread(i):
                act.wait_ge(sum_done, i + 1)
                wait(act, norm_done, i)
                act.activation(rec[:, :, :], side_ps[:, 0:ST * PW].rearrange("p (c n) -> p c n", c=ST),
                               ACT.Copy).then_inc(sum_evac, 1)

            def y_transposed(i):
                act.wait_ge(yt_done, i + 1)
                act.activation(yT_hi[:, :, bass.ds(i * PW, PW)], side_ps[:, 0:KD * PW].rearrange("p (k n) -> p k n", k=KD),
                               ACT.Copy).then_inc(yhi_done, 1)

            def load_matrix(i):
                wait(act, welo_done, i)
                act.dma_start(w_raw[:, :, :], a["we"][bass.ds(i, 1)].squeeze(0)).then_inc(wraw_in, 16)

            def expert_hi(i):
                act.wait_ge(wraw_in, 16 * i + 16)
                act.activation(we_hi[:, bass.ds(i, 1), :, :].squeeze(1), w_raw[:, :, :], ACT.Copy).then_inc(wehi_done, 1)

            def load_xq(i):
                wait(act, xn_done, i)
                act.dma_start(xq[0:PW, :], a["x"][bass.ds(i * PW, PW), :]).then_inc(xq_in, 16)

            def load_xr(i):
                wait(act, x1_done, i)
                act.dma_start(xr[0:PW, :], a["x"][bass.ds(i * PW, PW), :]).then_inc(xr_in, 16)

            def store_x1(i):
                act.wait_ge(x1_done, i + 1)
                act.dma_start(x1_dram[bass.ds(i * PW, PW), :], x1[0:PW, :]).then_inc(x1_out, 16)

            def pair(i, first=False, final=False):
                for c in range(PC):
                    q, j = divmod(c, GC)
                    if c == 0 and not final:
                        load_xq(i + 1)
                    exps(i, c)
                    if j < KD and not (final and q == PG - 1):
                        k_hi_evac(i * PG + q + 1, j, (q + 1) % 2)
                    if (q, j) == (0, 2) and not first:
                        sums_spread(i - 1)
                    if (q, j) == (0, 3):
                        expert_hi(i)
                    if (q, j) == (1, 2) and not final:
                        x_transposed(i + 1)
                    if (q, j) == (3, 3):
                        if not first:
                            store_x1(i - 1)
                        load_xr(i)
                        if not final:
                            load_matrix(i + 1)
                    if (q, j) == (4, 2) and not first:
                        y_transposed(i - 1)

            act.dma_start(gates[:, 0:1], bcast(a["g_xattn"], P)).then_inc(t_in, 16)
            act.dma_start(gates[:, 1:2], bcast(a["g_ffn"], P)).then_inc(t_in, 16)
            act.dma_start(gates[:, 2:3], bcast(a["rscale"], P)).then_inc(t_in, 16)
            for dst, src in ((ident, "ident"), (sumsel, "sumsel"), (rev_e, "rev_e")):
                act.dma_start(dst[:, :], a[src]).then_inc(t_in, 16)
            for dst, src in ((bo, "bo"), (gam, "gamma"), (bet, "beta")):
                act.dma_start(dst[:, :], bcast(a[src], P)).then_inc(t_in, 16)
            act.dma_start(wo[:, :, :], a["wo"]).then_inc(t_in, 16)
            act.dma_start(wr[:, :, :], a["wr"]).then_inc(wr_split, 16)
            load_matrix(0)
            act.wait_ge(t_in, 16 * N_T)
            act.activation(tg[:, :], gates[:, 0:2], ACT.Tanh).then_inc(tanh_done, 1)
            x_transposed(0)
            act.wait_ge(w_in, 16 * N_W)
            for m in range(KD):
                k_hi_evac(0, m, 0)
            act.wait_ge(m_ready, 2)
            pair(0, first=True)
            with act.Fori(1, NP - 1) as i:
                pair(i)
            pair(NP - 1, final=True)

            def second_of_two(part):
                cols = slice(0, RT) if part == 0 else slice(RT, NT)
                act.wait_ge(diff_done, part + 1)
                act.activation(e21[:, cols], e21[:, cols], ACT.Exp).then_inc(e21_done, 1)

            def hidden(f, first=False):
                for e in range(NE):
                    u = f * NE + e
                    act.wait_ge(fc_done, u + 1)
                    if not (first and e < 2):
                        act.wait_ge(sq_done, u - 1)
                    act.activation(h_relu[:, e % 2, :, :], sc_ps[:, e % 2, :].rearrange("p (m n) -> p m n", m=KD),
                                   ACT.Relu).then_inc(relu_done, 1)
                    act.wait_ge(sq_done, u + 1)
                    if not (first and e < NB):
                        act.wait_ge(y2_done, u - NB + 1)
                    act.activation(h_hi[:, e % NB, :, :], h_sq[:, e % 2, :, :], ACT.Copy).then_inc(hhi_done, 1)
                    if first and e == 3:
                        y_transposed(NP - 1)

            sums_spread(NP - 1)
            second_of_two(0)
            store_x1(NP - 1)
            hidden(0, first=True)
            second_of_two(1)
            with act.Fori(1, NF) as f:
                hidden(f)
            act.wait_ge(x1_out, 16 * NP)

        @block.vector
        def _(dve):
            seq = [0]

            def then(ins):
                seq[0] += 1
                ins.then_inc(dve_seq, 1)
                dve.wait_ge(dve_seq, seq[0])

            def statistics(ln, i, src):
                dve.bn_stats(st6[ln][0:PW, :], src[0:PW, :]).then_inc(ln_step[ln], 1)
                dve.wait_ge(ln_step[ln], 2 * i + 1)
                dve.memset(held[ln][:, :], 0.0)
                dve.bn_aggr(mv[ln][0:PW, :], st6[ln][0:PW, :]).then_inc(ln_step[ln], 1)
                dve.wait_ge(ln_step[ln], 2 * i + 2)
                dve.tensor_scalar(var_e[ln][0:PW, :], mv[ln][0:PW, 1:2], EPS, None, ALU.add).then_inc(var_done[ln], 1)

            def normalised(ln, i, dst, src):
                dve.wait_ge(rstd_done[ln], i + 1)
                return dve.tensor_scalar(dst[0:PW, :], src[0:PW, :], mv[ln][0:PW, 0:1], rstd[ln][0:PW, :],
                                         ALU.subtract, ALU.mult)

            def k_lo_evac(n, m, s):
                for half in range(2):
                    dve.wait_ge(k_hi, 2 * KD * n + 2 * m + half + 1)
                    rows, other = slice(half * 64, half * 64 + 64), slice(64 - half * 64, 128 - half * 64)
                    dve.scalar_tensor_tensor(kst[other, s, 2 * m + half, :], k_ps[rows, m, 0:TG], bk[rows, m:m + 1],
                                             plain(kst[rows, s, 2 * m + half, :]), ALU.add, ALU.subtract).then_inc(k_lo, 1)

            def v_evac_step(n, j, s):
                dve.wait_ge(vproj_done, n * GC + j + 1)
                if j == 0:
                    wait(dve, pv_done, (n - 1) * GC)
                dve.tensor_tensor(vst[0:TC, s, j, :, 0:HD], v_ps[0:TC, 0:D].rearrange("p (h d) -> p h d", h=NH),
                                  bv[0:TC, :].rearrange("p (h d) -> p h d", h=NH), ALU.add).then_inc(v_evac, 1)

            def q_evac(i):
                dve.wait_ge(qp_done, i + 1)
                wait(dve, q_step, 4 * i)
                for half in range(2):
                    src = slice(half * HW, (half + 1) * HW)
                    for copy in range(2):
                        dve.tensor_tensor(qT[copy * HW:(copy + 1) * HW, half:ST:2, :],
                                          side_ps[src, 0:KD * PW].rearrange("p (m n) -> p m n", m=KD),
                                          bq[src, :].unsqueeze(2).to_broadcast([HW, KD, PW]), ALU.add).then_inc(qT_done, 1)

            def q_split(i, b):
                n = 2 * i + b
                src = qT[:, :, b * S:(b + 1) * S]
                dve.wait_ge(qT_done, 4 * (i + 1))
                wait(dve, q_ready, 2 * n)
                dve.tensor_copy(q_rnd[:, :, :], src).then_inc(q_step, 1)
                dve.wait_ge(q_step, 2 * n + 1)
                dve.tensor_tensor(q_rem[:, :, :], src, plain(q_rnd[:, :, :]), ALU.subtract).then_inc(q_step, 1)

            def q_high(i, b):
                n = 2 * i + b
                dve.wait_ge(q_step, 2 * n + 2)
                wait(dve, scores_done, NC * (n - 1))
                q_diagonal(q_hi, b, plain(q_rnd[:, :, :]))

            def q_low(i, b):
                dve.wait_ge(q_step, 2 * (2 * i + b) + 2)
                q_diagonal(q_lo, b, q_rem[:, :, :])

            def q_diagonal(dst, b, part):
                shape = [P, ST, HS, S]
                dve.tensor_tensor(dst[:, b, :, :, :], part.unsqueeze(2).to_broadcast(shape),
                                  hmask[:, :].unsqueeze(1).unsqueeze(3).to_broadcast(shape), ALU.mult).then_inc(q_ready, 1)

            def o_evac_step(i, b):
                dve.wait_ge(pv_done, NC * (2 * i + b + 1))
                if b == 0:
                    wait(dve, op_done, i)
                dve.tensor_copy(ctxo[:, :, b * S:(b + 1) * S],
                                o_ps[:, 0:ST * S].rearrange("p (c n) -> p c n", c=ST)).then_inc(o_evac, 1)

            def inverse(i, col):
                dve.wait_ge(sum_evac, i + 1)
                dve.reciprocal(rec[:, col, :], rec[:, col, :]).then_inc(rec_done, 1)

            def divide(i):
                dve.wait_ge(rec_done, ST * (i + 1))
                dve.tensor_tensor(ctxo[:, :, :], ctxo[:, :, :], rec[:, :, :], ALU.mult).then_inc(norm_done, 1)

            def delta(i):
                dve.wait_ge(op_done, i + 1)
                dve.scalar_tensor_tensor(dlt[0:PW, :], side_ps[0:PW, 0:D], rs[0:PW, 0:1], bo[0:PW, :],
                                         ALU.mult, ALU.add).then_inc(dlt_evac, 1)

            def delta_statistics(i):
                dve.wait_ge(dlt_evac, i + 1)
                statistics(1, i, dlt)

            def x_after(i):
                normalised(1, i, dlt, dlt).then_inc(x1_step, 1)
                dve.wait_ge(x1_step, 2 * i + 1)
                dve.tensor_tensor(dlt[0:PW, :], dlt[0:PW, :], gam[0:PW, :], ALU.mult).then_inc(x1_step, 1)
                dve.wait_ge(x1_step, 2 * i + 2)
                dve.wait_ge(xb_done, i + 1)
                wait(dve, x1_out, 16 * i)
                dve.tensor_tensor(x1[0:PW, :], dlt[0:PW, :], xr[0:PW, :], ALU.add).then_inc(x1_done, 1)

            def x_after_statistics(i):
                dve.wait_ge(x1_done, i + 1)
                statistics(2, i, x1)

            def y_low(i):
                dve.wait_ge(yhi_done, i + 1)
                dve.tensor_tensor(yT_lo[:, :, bass.ds(i * PW, PW)], side_ps[:, 0:KD * PW].rearrange("p (k n) -> p k n", k=KD),
                                  plain(yT_hi[:, :, bass.ds(i * PW, PW)]), ALU.subtract).then_inc(ylo_done, 1)

            def pair(i, first=False, final=False):
                for c in range(PC):
                    q, j = divmod(c, GC)
                    n = i * PC + c
                    dve.wait_ge(exp_done, n + 1)
                    p = prob[0:TC, c % PB, :]
                    dve.tensor_scalar(p, p, EXP_LO, EXP_HI, ALU.max, ALU.min).then_inc(clip_done, 1)
                    if j == 0:
                        beside(i, q, j, first, final)
                    if not (final and q == PG - 1):
                        v_evac_step(i * PG + q + 1, j, (q + 1) % 2)
                        if j < KD:
                            k_lo_evac(i * PG + q + 1, j, (q + 1) % 2)
                    if j > 0:
                        beside(i, q, j, first, final)

            def beside(i, q, j, first, final):
                at = (q, j)
                if at == (0, 0):
                    if not first:
                        o_evac_step(i - 1, 1)
                    q_split(i, 1)
                if at == (0, 2):
                    q_high(i, 1)
                if at == (0, 3):
                    if not final:
                        dve.wait_ge(xq_in, 16 * (i + 2))
                        statistics(0, i + 1, xq)
                    if not first:
                        inverse(i - 1, 0)
                if at == (1, 0):
                    if not final:
                        normalised(0, i + 1, xn, xq).then_inc(xn_done, 1)
                    if not first:
                        inverse(i - 1, 1)
                if at == (1, 2):
                    q_low(i, 1)
                if at == (1, 3) and not first:
                    inverse(i - 1, 2)
                if at == (2, 0) and not first:
                    inverse(i - 1, 3)
                    divide(i - 1)
                if at == (2, 2) and not first:
                    delta(i - 1)
                if at == (2, 3) and not first:
                    delta_statistics(i - 1)
                if at == (3, 0):
                    o_evac_step(i, 0)
                    if not first:
                        x_after(i - 1)
                if at == (3, 2) and not final:
                    q_evac(i + 1)
                if at == (3, 3) and not first:
                    x_after_statistics(i - 1)
                if at == (4, 0):
                    if not first:
                        normalised(2, i - 1, dlt, x1).then_inc(y_done, 1)
                    if not final:
                        q_split(i + 1, 0)
                if at == (4, 2) and not first:
                    y_low(i - 1)
                if at == (4, 3) and not final:
                    q_high(i + 1, 0)
                if at == (5, 2) and not final:
                    q_low(i + 1, 0)

            dve.memset(o_ps[:, :], 0.0).then_inc(o_clear, 1)
            dve.wait_ge(xq_in, 16)
            statistics(0, 0, xq)
            normalised(0, 0, xn, xq).then_inc(xn_done, 1)
            dve.wait_ge(w_in, 16 * N_W)
            for src, dst in ((wk, wk_hi), (wv, wv_hi)):
                dve.tensor_copy(dst[:, :, :], src[:, :, :]).then_inc(w_split, 1)
            dve.wait_ge(w_split, 2)
            for src, hi, lo in ((wk, wk_hi, wk_lo), (wv, wv_hi, wv_lo)):
                dve.tensor_tensor(lo[:, :, :], src[:, :, :], plain(hi[:, :, :]), ALU.subtract).then_inc(w_split, 1)
            dve.tensor_scalar(m_scale[0:TC, :], mask_i[0:TC, :], 0.5, SCALE, ALU.is_gt, ALU.mult).then_inc(m_ready, 1)
            dve.wait_ge(m_ready, 1)
            dve.tensor_scalar(m_bias[0:TC, :], m_scale[0:TC, :], CLIP / SCALE, -CLIP, ALU.mult, ALU.add).then_inc(m_ready, 1)
            dve.wait_ge(tanh_done, 1)
            dve.tensor_scalar(rs[:, :], gates[:, 2:3], 0.0, RES_SCALE_MAX, ALU.max, ALU.min).then_inc(scale_done, 1)
            dve.wait_ge(scale_done, 1)
            for t, by in ((bo, rs[:, 0:1]), (gam, tg[:, 0:1]), (bet, tg[:, 0:1])):
                dve.tensor_scalar(t[:, :], t[:, :], by, None, ALU.mult).then_inc(scale_done, 1)
            dve.wait_ge(ones_done, 3)
            for m in range(KD):
                k_lo_evac(0, m, 0)
            for j in range(GC):
                v_evac_step(0, j, 0)
            q_evac(0)
            q_split(0, 0)
            q_high(0, 0)
            q_low(0, 0)
            dve.wait_ge(wr_split, 16)
            dve.tensor_copy(wr_hi[:, :, :], wr[:, :, :]).then_inc(wr_split, 1)
            dve.wait_ge(wr_split, 17)
            dve.tensor_tensor(wr_lo[:, :, :], wr[:, :, :], plain(wr_hi[:, :, :]), ALU.subtract).then_inc(wr_split, 1)
            dve.wait_ge(scale_done, 4)
            pair(0, first=True)
            with dve.Fori(1, NP - 1) as i:
                pair(i)
            pair(NP - 1, final=True)
            o_evac_step(NP - 1, 1)
            for col in range(ST):
                inverse(NP - 1, col)
            divide(NP - 1)

            def route(part):
                t0, t1 = (0, RT) if part == 0 else (RT, NT)
                per_tile = [P, t1 - t0, NE]
                revs = rev_e[:, :].unsqueeze(1).to_broadcast(per_tile)
                lg, ht, p1, p2 = (b[:, t0:t1, :] for b in (logit, hit, pick1, pick2))

                def over_e(b):
                    return b[:, t0:t1].unsqueeze(2).to_broadcast(per_tile)

                def largest(top, pick):
                    then(dve.tensor_reduce(top[:, t0:t1], lg, AX.X, ALU.max))
                    then(dve.tensor_tensor(ht, lg, over_e(top), ALU.is_equal))
                    then(dve.tensor_tensor(ht, ht, revs, ALU.mult))
                    then(dve.tensor_reduce(firstof[:, t0:t1], ht, AX.X, ALU.max))
                    then(dve.tensor_tensor(pick, revs, over_e(firstof), ALU.is_equal))

                dve.wait_ge(lg_done, t1)
                then(dve.tensor_copy(lg, logit_ps[part][:, t0 * NE:t1 * NE].rearrange("p (t e) -> p t e", e=NE)))
                largest(top1, p1)
                then(dve.scalar_tensor_tensor(lg, p1, -BIG, lg, ALU.mult, ALU.add))
                largest(top2, p2)
                dve.tensor_tensor(e21[:, t0:t1], top2[:, t0:t1], top1[:, t0:t1], ALU.subtract).then_inc(diff_done, 1)
                dve.wait_ge(e21_done, part + 1)
                then(dve.tensor_scalar(pr2[:, t0:t1], e21[:, t0:t1], 1.0, None, ALU.add))
                then(dve.reciprocal(pr1[:, t0:t1], pr2[:, t0:t1]))
                then(dve.tensor_scalar(pr1[:, t0:t1], pr1[:, t0:t1], tg[:, 1:2], None, ALU.mult))
                then(dve.tensor_tensor(pr2[:, t0:t1], pr1[:, t0:t1], e21[:, t0:t1], ALU.mult))
                dve.tensor_tensor(p1, p1, over_e(pr1), ALU.mult)
                then(dve.tensor_tensor(p2, p2, over_e(pr2), ALU.mult))
                then(dve.tensor_tensor(w_tok[:, t0:t1, :], p1, p2, ALU.add))

            def accumulate(f, e):
                u = f * NE + e
                dve.wait_ge(y2_done, u + 1)
                for t in range(2):
                    tile = f * 2 + t
                    if e > 0:
                        dve.wait_ge(acc_done, 2 * u - 1 + t)
                    total = acc[:, bass.ds(tile, 1), :].squeeze(1)
                    dve.scalar_tensor_tensor(total, sc_ps[:, 2 + e % 2, t * D:(t + 1) * D],
                                             w_tok[:, bass.ds(tile, 1), e], total, ALU.mult, ALU.add).then_inc(acc_done, 1)

            def experts(f, first=False):
                for e in range(NE):
                    u = f * NE + e
                    dve.wait_ge(relu_done, u + 1)
                    if not (first and e < 2):
                        dve.wait_ge(hlo_done, u - 1)
                    r = h_relu[:, e % 2, :, :]
                    dve.tensor_tensor(h_sq[:, e % 2, :, :], r, r, ALU.mult).then_inc(sq_done, 1)
                    if e >= 2:
                        accumulate(f, e - 2)
                    elif not first:
                        accumulate(f - 1, NE - 2 + e)
                    if first and e == 3:
                        y_low(NP - 1)
                if first:
                    route(1)

            route(0)
            delta(NP - 1)
            delta_statistics(NP - 1)
            x_after(NP - 1)
            x_after_statistics(NP - 1)
            normalised(2, NP - 1, dlt, x1).then_inc(y_done, 1)
            dve.wait_ge(acc_in[0], 16)
            experts(0, first=True)
            dve.wait_ge(acc_in[1], 16)
            with dve.Fori(1, NF) as f:
                experts(f)
            accumulate(NF - 1, NE - 2)
            accumulate(NF - 1, NE - 1)


def kernel(x, ctx_2048, mask_BxS2_ik0, g_xattn, g_ffn, L0_xattn_Wq, L0_xattn_bq, L0_xattn_Wk, L0_xattn_bk,
           L0_xattn_Wv, L0_xattn_bv, L0_xattn_Wo, L0_xattn_bo, L0_xattn_ln_gamma, L0_xattn_ln_beta,
           L0_xattn_residual_scale, L0_ffn_w_router, L0_ffn_w_fc, L0_ffn_w_proj):
    import numpy as np
    import concourse.bacc as bacc
    from concourse.bass_utils import run_bass_kernel_spmd

    def rows(w):
        w = np.asarray(w)
        w = w.reshape(w.shape[:-2] + (KD, P, w.shape[-1]))
        return np.ascontiguousarray(np.moveaxis(w, -3, -2))

    def row(v):
        return np.ascontiguousarray(np.asarray(v).reshape(1, -1))

    ctxT = np.asarray(ctx_2048).reshape(B * NG, TG, KD, P).transpose(0, 3, 2, 1)
    wo = np.zeros((ST, 32, ST, D), np.float32)
    wo[:, 0:HD] = np.asarray(L0_xattn_Wo).T.reshape(ST, ST, HD, D).transpose(1, 2, 0, 3)
    r = np.arange(P)
    arrays = {
        "x": np.ascontiguousarray(np.asarray(x).reshape(TOK, D)),
        "ctxT": np.ascontiguousarray(ctxT),
        "mask": np.ascontiguousarray(np.asarray(mask_BxS2_ik0).reshape(B * NC, TC).T),
        "wk": rows(np.asarray(L0_xattn_Wk).T), "wv": rows(np.asarray(L0_xattn_Wv).T), "wq": rows(np.asarray(L0_xattn_Wq).T),
        "wo": wo.reshape(P, ST, D), "wr": rows(L0_ffn_w_router), 
        "we": np.ascontiguousarray(np.stack([rows(L0_ffn_w_fc), rows(L0_ffn_w_proj)], 1).reshape(NW, P, KD, D)),
        "bk": np.ascontiguousarray(np.asarray(L0_xattn_bk).reshape(KD, P).T),
        "bq": np.ascontiguousarray(np.asarray(L0_xattn_bq).reshape(KD, P).T),
        "bv": row(L0_xattn_bv), "bo": row(L0_xattn_bo), "gamma": row(L0_xattn_ln_gamma), "beta": row(L0_xattn_ln_beta),
        "g_xattn": row(g_xattn), "g_ffn": row(g_ffn), "rscale": row(L0_xattn_residual_scale),
        "ident": np.eye(P, dtype=np.float32),
        "sumsel": (r[:, None] == r[None, :] // 32 * 32 + HD).astype(np.float32),
        "hmask": (r[:, None] % HW // HD == np.arange(HS)[None, :]).astype(np.float32),
        "rev_e": np.tile(NE - np.arange(NE, dtype=np.float32), (P, 1)),
    }
    nc = bacc.Bacc("TRN2", target_bir_lowering=False, num_devices=1)
    args = {k: nc.dram_tensor(f"in_{k}", v.shape, mybir.dt.from_np(v.dtype), kind="ExternalInput").ap()
            for k, v in arrays.items()}
    out = nc.dram_tensor("out_y", (P, NT, D), mybir.dt.float32, kind="ExternalOutput").ap()
    x1_dram = nc.dram_tensor("x1_scratch", (TOK, D), mybir.dt.float32, kind="Internal").ap()
    gated_cross_attention_moe(nc, args, x1_dram, out)
    got = run_bass_kernel_spmd(nc, [{f"in_{k}": v for k, v in arrays.items()}], core_ids=[0])
    y = got.results[0]["out_y"]
    return np.ascontiguousarray(y.transpose(1, 0, 2)).reshape(B, S, D)
```

```python
import concourse.bass as bass
from concourse import mybir
from contextlib import ExitStack

B, S, D, T = 32, 56, 256, 1500
NH, HD = 16, 16
P = 128
KD = D // P
TC = 125
GC = 4
TG = TC * GC
NG = T // TG
NC = NG * GC
TOK = B * S
NT = TOK // P
NP = B // 2
PW = 2 * S
PG = 2 * NG
PC = 2 * NC
RT = 12
ST = 4
HS = NH // ST
HW = HS * HD
NE = 8
FT = 256
NF = TOK // FT
VW = HD + 1
PV = 3
PB = PV + 1
NW = 2 * NE
NB = 4
CST = (P, P, NE, HS, KD, KD)
EPS = 1e-5
CLIP = 50.0
EXP_HI = 5.184705528587072e21
EXP_LO = 1.9287498479639178e-22
BIG = 3.0e38
SCALE = HD ** -0.5
RES_SCALE_MAX = 0.3


def gated_cross_attention_moe(nc, a, x1_dram, out):
    fp32, fp32r, i32 = mybir.dt.float32, mybir.dt.float32r, mybir.dt.int32
    ALU = mybir.AluOpType
    ACT = mybir.ActivationFunctionType
    AX = mybir.AxisListType

    with ExitStack() as ctx:
        def sem(name):
            return ctx.enter_context(nc.semaphore(name))

        def sb(name, shape, dt=fp32, scope=ctx):
            return scope.enter_context(nc.sbuf_tensor(name, shape, dt))

        def plain(ap):
            return ap.bitcast(fp32)

        def wait(eng, s, value):
            if not isinstance(value, int) or value > 0:
                eng.wait_ge(s, value)

        def step(f, e):
            return f * NE + e if isinstance(f, int) else None

        yT_hi = sb("yT_hi", [P, KD, TOK], fp32r)
        yT_lo = sb("yT_lo", [P, KD, TOK], fp32r)
        we_hi = sb("we_hi", [P, NW, KD, D], fp32r)
        we_lo = sb("we_lo", [P, NW, KD, D], fp32r)
        w_raw = sb("w_raw", [P, KD, D])
        wo = sb("wo", [P, KD, D])
        wr = sb("wr", [P, KD, NE])
        wr_2 = sb("wr_2", [P, KD, 2, NE], fp32r)
        cst = sb("cst", [P, sum(CST)])
        ident, sumsel, rev_e, hmask, bk, bq = (cst[:, sum(CST[:i]):sum(CST[:i + 1])] for i in range(len(CST)))
        rowv = sb("rowv", [P, 4 * D + 3])
        bv, bo, gam, bet = (rowv[:, i * D:(i + 1) * D] for i in range(4))
        gates = rowv[:, 4 * D:4 * D + 3]
        tg = sb("tg", [P, 2])
        rs = sb("rs", [P, 1])
        held = [sb(f"held_{i}", [P, 1]) for i in range(3)]
        xq = sb("xq", [P, D])
        xn = sb("xn", [P, D])
        xr = sb("xr", [P, D])
        dlt = sb("dlt", [P, D])
        x1 = sb("x1", [P, D])
        ctxo = sb("ctxo", [P, ST, PW])
        sum_hi = sb("sum_hi", [P, ST, PW], fp32r)
        sum_lo = sb("sum_lo", [P, ST, PW], fp32r)
        sumsel_r = sb("sumsel_r", [P, P], fp32r)
        rec = sb("rec", [P, ST, PW])
        mhalf = sb("mhalf", [P, 1])
        st6 = [sb(f"st6_{i}", [P, 6]) for i in range(3)]
        mv = [sb(f"mv_{i}", [P, 2]) for i in range(3)]
        var_e = [sb(f"var_e_{i}", [P, 1]) for i in range(3)]
        rstd = [sb(f"rstd_{i}", [P, 1]) for i in range(3)]

        att = ExitStack()
        wk_hi = sb("wk_hi", [P, KD, D], fp32r, scope=att)
        wk_lo = sb("wk_lo", [P, KD, D], fp32r, scope=att)
        wv_hi = sb("wv_hi", [P, KD, D], fp32r, scope=att)
        wv_lo = sb("wv_lo", [P, KD, D], fp32r, scope=att)
        wq = sb("wq", [P, KD, D], scope=att)
        m_scale = sb("m_scale", [P, B * NC], scope=att)
        m_bias = sb("m_bias", [P, B * NC], scope=att)
        one = sb("one", [P, KD], scope=att)
        xnT = sb("xnT", [P, KD, PW], scope=att)
        qT = sb("qT", [P, ST, PW], scope=att)
        raw = sb("raw", [P, 2, KD, TG], scope=att)
        c_hi = sb("c_hi", [P, 2, KD, TG], fp32r, scope=att)
        c_lo = sb("c_lo", [P, 2, KD, TG], fp32r, scope=att)
        kst = sb("kst", [P, 2, ST, TG], fp32r, scope=att)
        vst = sb("vst", [P, 2, GC, NH, VW], scope=att)
        q_rnd = sb("q_rnd", [P, ST, S], fp32r, scope=att)
        q_rem = sb("q_rem", [P, ST, S], scope=att)
        q_hi = sb("q_hi", [P, 2, ST, HS, S], fp32r, scope=att)
        q_lo = sb("q_lo", [P, 2, ST, HS, S], fp32r, scope=att)
        early = ExitStack()
        wk = sb("wk", [P, KD, D], scope=early)
        wv = sb("wv", [P, KD, D], scope=early)
        mask_i = sb("mask_i", [P, B * NC], i32, scope=early)
        early.close()
        prob = sb("prob", [P, PB, NH * S], scope=att)
        att.close()

        ffn = ExitStack()
        logit = sb("logit", [P, NT, NE], scope=ffn)
        hit = sb("hit", [P, NT, NE], scope=ffn)
        pick1 = sb("pick1", [P, NT, NE], scope=ffn)
        pick2 = sb("pick2", [P, NT, NE], scope=ffn)
        w_tok = sb("w_tok", [P, NT, NE], scope=ffn)
        top1 = sb("top1", [P, NT], scope=ffn)
        top2 = sb("top2", [P, NT], scope=ffn)
        firstof = sb("firstof", [P, NT], scope=ffn)
        e21 = sb("e21", [P, NT], scope=ffn)
        pr1 = sb("pr1", [P, NT], scope=ffn)
        pr2 = sb("pr2", [P, NT], scope=ffn)
        acc = sb("acc", [P, NT, D], scope=ffn)
        h_relu = sb("h_relu", [P, 2, KD, FT], scope=ffn)
        h_sq = sb("h_sq", [P, 2, KD, FT], scope=ffn)
        h_hi = sb("h_hi", [P, NB, KD, FT], fp32r, scope=ffn)
        h_lo = sb("h_lo", [P, NB, KD, FT], fp32r, scope=ffn)
        ffn.close()

        sc_ps = ctx.enter_context(nc.psum_tensor("sc_ps", [P, 4, 512], fp32))
        k_ps = ctx.enter_context(nc.psum_tensor("k_ps", [P, KD, 512], fp32))
        v_ps = ctx.enter_context(nc.psum_tensor("v_ps", [P, 512], fp32))
        o_ps = ctx.enter_context(nc.psum_tensor("o_ps", [P, 512], fp32))
        side_ps = k_ps[:, 0, :]
        logit_ps = [k_ps[:, 1, :], o_ps[:, :]]

        first_side = sc_ps[:, 0, :]
        first_v = [v_ps[:, :], sc_ps[:, 2, :], sc_ps[:, 3, :], o_ps[:, :]]

        def v_bank(n, j):
            return first_v[j] if isinstance(n, int) and n == 0 else v_ps

        cst_in = sem("cst_in")
        row_in = sem("row_in")
        mask_in = sem("mask_in")
        wk_in = sem("wk_in")
        wq_in = sem("wq_in")
        wv_in = sem("wv_in")
        wo_in = sem("wo_in")
        ones_done = sem("ones_done")
        o_clear = sem("o_clear")
        whi_done = sem("whi_done")
        wlo_done = sem("wlo_done")
        m_ready = sem("m_ready")
        tanh_done = sem("tanh_done")
        scale_done = sem("scale_done")
        wr_split = sem("wr_split")
        raw_in = [sem(f"raw_in{i}") for i in range(2)]
        ctx_hi = sem("ctx_hi")
        ctx_split = sem("ctx_split")
        kproj_done = sem("kproj_done")
        vproj_done = sem("vproj_done")
        k_hi = sem("k_hi")
        k_lo = sem("k_lo")
        v_evac = sem("v_evac")
        q_step = sem("q_step")
        q_ready = sem("q_ready")
        scores_done = sem("scores_done")
        exp_done = sem("exp_done")
        clip_done = sem("clip_done")
        pv_done = sem("pv_done")
        o_evac = sem("o_evac")
        sum_split = sem("sum_split")
        sel_done = sem("sel_done")
        xq_in = sem("xq_in")
        xn_done = sem("xn_done")
        xt_done = sem("xt_done")
        xT_done = sem("xT_done")
        qp_done = sem("qp_done")
        qT_done = sem("qT_done")
        xr_in = sem("xr_in")
        xb_done = sem("xb_done")
        sum_done = sem("sum_done")
        sum_evac = sem("sum_evac")
        rec_done = sem("rec_done")
        norm_done = sem("norm_done")
        packed = sem("packed")
        op_done = sem("op_done")
        dlt_evac = sem("dlt_evac")
        x1_step = sem("x1_step")
        x1_done = sem("x1_done")
        x1_out = sem("x1_out")
        y_done = sem("y_done")
        yt_done = sem("yt_done")
        yhi_done = sem("yhi_done")
        ylo_done = sem("ylo_done")
        ln_step = [sem(f"ln_step{i}") for i in range(3)]
        var_done = [sem(f"var_done{i}") for i in range(3)]
        rstd_done = [sem(f"rstd_done{i}") for i in range(3)]
        wraw_in = sem("wraw_in")
        wehi_done = sem("wehi_done")
        welo_done = sem("welo_done")
        lg_done = sem("lg_done")
        diff_done = sem("diff_done")
        e21_done = sem("e21_done")
        acc_in = [sem(f"acc_in{i}") for i in range(3)]
        fc_done = sem("fc_done")
        relu_done = sem("relu_done")
        sq_done = sem("sq_done")
        hhi_done = sem("hhi_done")
        hlo_done = sem("hlo_done")
        y2_done = sem("y2_done")
        acc_done = sem("acc_done")
        out_done = sem("out_done")
        dve_seq = sem("dve_seq")

        block = ctx.enter_context(nc.Block())

        def bcast(ap, n):
            return ap.partition_broadcast(n)

        @block.sync
        def _(sp):
            sp.dma_start(raw[:, 0, :, :], a["ctxT"][0]).then_inc(raw_in[0], 16)
            sp.dma_start(cst[:, :], a["cst"]).then_inc(cst_in, 16)
            sp.dma_start(wv[:, :, :], a["wv"]).then_inc(wv_in, 16)
            sp.dma_start(mask_i[0:TC, :], a["mask"]).then_inc(mask_in, 16)
            sp.dma_start(raw[:, 1, :, :], a["ctxT"][1]).then_inc(raw_in[1], 16)
            sp.dma_start(wr[:, :, :], a["wr"]).then_inc(wr_split, 16)
            sp.dma_start(wo[:, :, :], a["wo"]).then_inc(wo_in, 16)

            def load_group(n, s):
                wait(sp, ctx_split, n - 1)
                sp.dma_start(raw[:, s, :, :], a["ctxT"][bass.ds(n, 1)].squeeze(0)).then_inc(raw_in[s], 16)

            def pack(i):
                sp.wait_ge(norm_done, i + 1)
                for q in range(ST):
                    sp.dma_start(rec[q * 32 + HD:q * 32 + 2 * HD, 0:ST:2, :],
                                 rec[q * 32:q * 32 + HD, 1:ST:2, :]).then_inc(packed, 16)

            for n in range(2, PG):
                load_group(n, n % 2)
            for q in range(PG):
                load_group(PG + q, q % 2)
            with sp.Fori(2, NP) as i:
                for q in range(PG):
                    load_group(i * PG + q, q % 2)
                    if q == 0:
                        pack(i - 2)
            pack(NP - 2)
            sp.wait_ge(pv_done, B * NC)
            for part, (t0, t1, pairs) in enumerate(((0, 2, NP - 1), (2, RT, NP - 1), (RT, NT, NP))):
                sp.wait_ge(x1_out, 16 * pairs)
                sp.dma_start(acc[:, t0:t1, :], x1_dram[t0 * P:t1 * P, :].rearrange("(t p) d -> p t d", p=P))\
                    .then_inc(acc_in[part], 16)
                if part == 0:
                    pack(NP - 1)
            for f in range(NF):
                sp.wait_ge(acc_done, 2 * NE * (f + 1))
                sp.dma_start(out[:, 2 * f:2 * f + 2, :], acc[:, 2 * f:2 * f + 2, :]).then_inc(out_done, 16)
            sp.wait_ge(out_done, 16 * NF)

        @block.gpsimd
        def _(pool):
            pool.memset(one[:, :], 1.0).then_inc(ones_done, 1)
            pool.memset(mhalf[:, :], -0.5).then_inc(ones_done, 1)
            pool.memset(vst[:, :, :, :, HD:VW], 1.0).then_inc(ones_done, 1)
            pool.wait_ge(ones_done, 3)

            def split(n, s, count):
                pool.wait_ge(raw_in[s], 16 * count)
                wait(pool, vproj_done, GC * (n - 1))
                r = raw[:, s, :, :]
                pool.tensor_tensor(c_hi[:, s, :, :], r, one[:, :].unsqueeze(2).to_broadcast([P, KD, TG]),
                                   ALU.mult).then_inc(ctx_hi, 1)
                pool.wait_ge(ctx_hi, n + 1)
                pool.tensor_tensor(c_lo[:, s, :, :], r, plain(c_hi[:, s, :, :]), ALU.subtract).then_inc(ctx_split, 1)

            def inv_std(ln, i):
                pool.wait_ge(var_done[ln], i + 1)
                pool.tensor_tensor(rstd[ln][0:PW, :], var_e[ln][0:PW, :], mhalf[0:PW, :], ALU.pow)\
                    .then_inc(rstd_done[ln], 1)

            def x_plus_beta(i):
                pool.wait_ge(xr_in, 16 * i + 16)
                pool.tensor_tensor(xr[0:PW, :], xr[0:PW, :], bet[0:PW, :], ALU.add).then_inc(xb_done, 1)

            def expert_lo(i):
                pool.wait_ge(wehi_done, i + 1)
                pool.tensor_tensor(we_lo[:, bass.ds(i, 1), :, :].squeeze(1), w_raw[:, :, :],
                                   plain(we_hi[:, bass.ds(i, 1), :, :].squeeze(1)), ALU.subtract).then_inc(welo_done, 1)

            def pair(i, first=False, final=False):
                for q in range(2, PG + 2):
                    if not (final and q >= PG):
                        split(i * PG + q, q % 2, (i * PG + q) // 2 + 1 if isinstance(i, int) else i * NG + q // 2 + 1)
                    if q == 2 and not final:
                        inv_std(0, i + 1)
                        expert_lo(i)
                    if q == 2 and final:
                        expert_lo(i)
                    if q == 5 and not first:
                        x_plus_beta(i - 1)
                        inv_std(1, i - 1)
                    if q == 6 and not first:
                        inv_std(2, i - 1)

            inv_std(0, 0)
            split(0, 0, 1)
            split(1, 1, 1)
            pool.wait_ge(scale_done, 4)
            pair(0, first=True)
            with pool.Fori(1, NP - 1) as i:
                pair(i)
            pair(NP - 1, final=True)

            def h_low(f):
                for e in range(NE):
                    u = f * NE + e
                    at = step(f, e)
                    pool.wait_ge(hhi_done, u + 1)
                    pool.tensor_tensor(h_lo[:, e % NB, :, :], h_sq[:, e % 2, :, :], plain(h_hi[:, e % NB, :, :]),
                                       ALU.subtract).then_inc(hlo_done, 1)
                    if at == 5:
                        x_plus_beta(NP - 1)
                        inv_std(1, NP - 1)
                    if at == 6:
                        inv_std(2, NP - 1)

            h_low(0)
            with pool.Fori(1, NF) as f:
                h_low(f)

        @block.tensor
        def _(pe):
            def mm3(ps, w_h, w_l, m_h, m_l, first, last):
                pe.matmul(ps, w_h, m_h, start=first, stop=False)
                pe.matmul(ps, w_h, m_l, start=False, stop=False)
                return pe.matmul(ps, w_l, m_h, start=False, stop=last)

            def k_proj(n, m, s, side=None):
                if m == 0:
                    pe.wait_ge(ctx_split, n + 1)
                if side:
                    wait(pe, *side)
                wait(pe, k_lo, 4 * n - 4 + 2 * m + 2)
                ws = slice(m * P, (m + 1) * P)
                for k in range(KD):
                    last = mm3(k_ps[:, m, 0:TG], wk_hi[:, k, ws], wk_lo[:, k, ws], c_hi[:, s, k, :], c_lo[:, s, k, :],
                               k == 0, k == KD - 1)
                last.then_inc(kproj_done, 1)

            def v_proj(n, j, s):
                if v_bank(n, j) is v_ps:
                    wait(pe, v_evac, n * GC + j)
                cs = slice(j * TC, (j + 1) * TC)
                for k in range(KD):
                    last = mm3(v_bank(n, j)[0:TC, 0:D], c_hi[:, s, k, cs], c_lo[:, s, k, cs], wv_hi[:, k, :], wv_lo[:, k, :],
                               k == 0, k == KD - 1)
                last.then_inc(vproj_done, 1)

            def scores(i, c):
                n = i * PC + c
                b, g = c // NC, c // GC
                if c % NC == 0:
                    pe.wait_ge(q_ready, 4 * i + 2 * b + 2)
                if c % GC == 0:
                    pe.wait_ge(k_lo, 4 * (i * PG + g + 1))
                wait(pe, exp_done, n - 1)
                cs = slice(c % GC * TC, (c % GC + 1) * TC)
                for st in range(ST):
                    ps = sc_ps[0:TC, 2 * (c % 2) + st // 2, st % 2 * HS * S:(st % 2 + 1) * HS * S]
                    k = kst[:, g % 2, st, cs]
                    pe.matmul(ps, k, q_hi[:, b, st, :, :], start=True, stop=False)
                    last = pe.matmul(ps, k, q_lo[:, b, st, :, :], start=False, stop=True)
                last.then_inc(scores_done, 1)

            def pv(i, c):
                n = i * PC + c
                if c % NC == 0:
                    wait(pe, o_evac, 2 * i + c // NC)
                if c % PV == 0:
                    pe.wait_ge(v_evac, n + PV)
                    pe.wait_ge(clip_done, n + PV)
                for h in range(NH):
                    col, q = divmod(h, ST)
                    last = pe.matmul(o_ps[q * 32:q * 32 + VW, col * S:(col + 1) * S], vst[0:TC, c // GC % 2, c % GC, h, :],
                                     prob[0:TC, c % PB, h * S:(h + 1) * S], start=(c % NC == 0 and col == 0),
                                     stop=(c % NC == NC - 1), skip_group_check=True)
                last.then_inc(pv_done, 1)

            def x_transpose(i, bank=side_ps):
                pe.wait_ge(xn_done, i + 1)
                for k in range(KD):
                    last = pe.transpose(bank[:, k * PW:(k + 1) * PW], xn[0:PW, k * P:(k + 1) * P], ident[0:PW, 0:PW])
                last.then_inc(xt_done, 1)

            def q_proj(i, bank=side_ps):
                pe.wait_ge(xT_done, i + 1)
                for m in range(KD):
                    for k in range(KD):
                        last = pe.matmul(bank[:, m * PW:(m + 1) * PW], wq[:, k, m * P:(m + 1) * P], xnT[:, k, :],
                                         start=(k == 0), stop=(k == KD - 1))
                last.then_inc(qp_done, 1)

            def spread_sums(i):
                pe.wait_ge(sum_split, 4 * i + 4)
                pe.matmul(side_ps[:, 0:ST * PW], sumsel_r[:, :], sum_hi[:, :, :], start=True, stop=False)
                pe.matmul(side_ps[:, 0:ST * PW], sumsel_r[:, :], sum_lo[:, :, :], start=False, stop=True).then_inc(sum_done, 1)

            def out_proj(i):
                pe.wait_ge(packed, 16 * ST * (i + 1))
                for k in range(KD):
                    last = pe.matmul(side_ps[0:PW, 0:D], rec[:, 2 * k, :], wo[:, k, :], start=(k == 0), stop=(k == KD - 1))
                last.then_inc(op_done, 1)

            def y_transpose(i):
                pe.wait_ge(y_done, i + 1)
                for k in range(KD):
                    last = pe.transpose(side_ps[:, k * PW:(k + 1) * PW], dlt[0:PW, k * P:(k + 1) * P], ident[0:PW, 0:PW])
                last.then_inc(yt_done, 1)

            def router(part, t):
                ts = slice(t * P, (t + 1) * P)
                both = logit_ps[part][:, t * 2 * NE:(t + 1) * 2 * NE]
                pe.matmul(both, yT_hi[:, 0, ts], wr_2[:, 0, :, :], start=True, stop=False, skip_group_check=True)
                for k in range(KD):
                    pe.matmul(both[:, 0:NE], yT_lo[:, k, ts], wr_2[:, k, 0, :], start=False, stop=False, skip_group_check=True)
                pe.matmul(both, yT_hi[:, 1, ts], wr_2[:, 1, :, :], start=False, stop=True, skip_group_check=True)\
                    .then_inc(lg_done, 1)

            def pair(i, first=False, final=False):
                freed = {}
                if not first:
                    freed.update({0: (sum_evac, i), 3: (dlt_evac, i)})
                if not final:
                    freed.update({1: (xT_done, i + 2), 2: (qT_done, 4 * (i + 2))})
                for c in range(PC):
                    q, j = divmod(c, GC)
                    more = not (final and q == PG - 1)
                    if first and c == 1:
                        pe.wait_ge(v_evac, 3)
                    if first and c == PV:
                        pe.wait_ge(o_clear, 1)
                    scores(i, c)
                    if (q, j) == (5, 3) and not first:
                        pe.wait_ge(ylo_done, i)
                    if more and j < KD:
                        k_proj(i * PG + q + 1, j, (q + 1) % 2, freed.get(q - 1) if j == 0 else None)
                    if more:
                        v_proj(i * PG + q + 1, j, (q + 1) % 2)
                    if c % PV == 0 and not (first and c == 0):
                        for d in range(PV, 0, -1):
                            if c > 0:
                                pv(i, c - d)
                            else:
                                pv(i - 1, PC - d)
                    if j == 2:
                        if more:
                            pe.wait_ge(k_lo, 4 * (i * PG + q + 1) + 2)
                        if q == 0 and not first:
                            spread_sums(i - 1)
                        if q == 1 and not final:
                            x_transpose(i + 1)
                        if q == 2 and not final:
                            q_proj(i + 1)
                        if q == 3 and not first:
                            out_proj(i - 1)
                    if (q, j) == (5, 1) and not first:
                        if more:
                            pe.wait_ge(k_lo, 4 * (i * PG + q + 1) + 2)
                        y_transpose(i - 1)
                    if final and (q, j) == (PG - 2, 3):
                        pe.wait_ge(ylo_done, NP - 2)
                        pe.wait_ge(wr_split, 18)
                        pe.wait_ge(k_lo, 4 * B * NG)
                        for t in range(RT):
                            router(0, t)

            pe.wait_ge(cst_in, 16)
            x_transpose(0, first_side)
            pe.wait_ge(wq_in, 16)
            q_proj(0, first_side)
            pe.wait_ge(wlo_done, 1)
            k_proj(0, 0, 0)
            k_proj(0, 1, 0)
            pe.wait_ge(wlo_done, 2)
            for j in range(GC):
                v_proj(0, j, 0)
            pair(0, first=True)
            pe.wait_ge(wo_in, 16)
            pe.wait_ge(sel_done, 1)
            with pe.Fori(1, NP - 1) as i:
                pair(i)
            pair(NP - 1, final=True)
            def fc(f, e):
                u = f * NE + e
                wait(pe, relu_done, u - 1)
                for m in range(KD):
                    ws = slice(m * P, (m + 1) * P)
                    for k in range(KD):
                        last = mm3(sc_ps[:, e % 2, m * FT:(m + 1) * FT], we_hi[:, 2 * e, k, ws], we_lo[:, 2 * e, k, ws],
                                   yT_hi[:, k, bass.ds(f * FT, FT)], yT_lo[:, k, bass.ds(f * FT, FT)], k == 0, k == KD - 1)
                last.then_inc(fc_done, 1)

            def proj(f, e):
                u = f * NE + e
                pe.wait_ge(hlo_done, u + 1)
                wait(pe, acc_done, 2 * u - 2)
                for t in range(2):
                    ts = slice(t * P, (t + 1) * P)
                    for k in range(KD):
                        last = mm3(sc_ps[:, 2 + e % 2, t * D:(t + 1) * D], h_hi[:, e % NB, k, ts], h_lo[:, e % NB, k, ts],
                                   we_hi[:, 2 * e + 1, k, :], we_lo[:, 2 * e + 1, k, :], k == 0, k == KD - 1)
                last.then_inc(y2_done, 1)

            def experts(f, first=False):
                for e in range(NE):
                    at = step(f, e)
                    if not (first and e == 0):
                        fc(f, e)
                    if at == 1:
                        spread_sums(NP - 1)
                    if e >= 2:
                        proj(f, e - 2)
                    elif not first:
                        proj(f - 1, NE - 2 + e)
                    if at == 5:
                        out_proj(NP - 1)
                    if at == 9:
                        y_transpose(NP - 1)
                    if at == 12:
                        pe.wait_ge(ylo_done, NP)
                        for t in range(RT, NT):
                            router(1, t)

            pe.wait_ge(welo_done, NW)
            pe.wait_ge(exp_done, B * NC - 1)
            fc(0, 0)
            for d in range(PV, 0, -1):
                pv(NP - 1, PC - d)
            experts(0, first=True)
            experts(1)
            with pe.Fori(2, NF) as f:
                experts(f)
            proj(NF - 1, NE - 2)
            proj(NF - 1, NE - 1)

        @block.scalar
        def _(act):
            def k_hi_evac(n, m, s):
                act.wait_ge(kproj_done, KD * n + m + 1)
                if m == 0:
                    wait(act, scores_done, GC * (n - 1))
                for half in range(2):
                    rows = slice(half * 64, half * 64 + 64)
                    act.activation(kst[rows, s, 2 * m + half, :], k_ps[rows, m, 0:TG], ACT.Identity,
                                   bias=bk[rows, m:m + 1]).then_inc(k_hi, 1)

            def exps(i, c):
                n = i * PC + c
                act.wait_ge(scores_done, n + 1)
                wait(act, pv_done, n - PB + 1)
                act.activation(prob[0:TC, c % PB, :].rearrange("p (c n) -> p c n", c=2),
                               sc_ps[0:TC, 2 * (c % 2):2 * (c % 2) + 2, 0:NH * S // 2], ACT.Exp,
                               scale=m_scale[0:TC, bass.ds(n, 1)], bias=m_bias[0:TC, bass.ds(n, 1)]).then_inc(exp_done, 1)

            def x_transposed(i, bank=side_ps):
                act.wait_ge(xt_done, i + 1)
                wait(act, qp_done, i)
                act.activation(xnT[:, :, :], bank[:, 0:KD * PW].rearrange("p (k n) -> p k n", k=KD),
                               ACT.Copy).then_inc(xT_done, 1)

            def sums_spread(i):
                act.wait_ge(sum_done, i + 1)
                wait(act, op_done, i)
                act.activation(rec[:, :, :], side_ps[:, 0:ST * PW].rearrange("p (c n) -> p c n", c=ST),
                               ACT.Copy).then_inc(sum_evac, 1)

            def y_transposed(i):
                act.wait_ge(yt_done, i + 1)
                act.activation(yT_hi[:, :, bass.ds(i * PW, PW)], side_ps[:, 0:KD * PW].rearrange("p (k n) -> p k n", k=KD),
                               ACT.Copy).then_inc(yhi_done, 1)

            def load_matrix(i):
                wait(act, welo_done, i)
                act.dma_start(w_raw[:, :, :], a["we"][bass.ds(i, 1)].squeeze(0)).then_inc(wraw_in, 16)

            def expert_hi(i):
                act.wait_ge(wraw_in, 16 * i + 16)
                act.activation(we_hi[:, bass.ds(i, 1), :, :].squeeze(1), w_raw[:, :, :], ACT.Copy).then_inc(wehi_done, 1)

            def load_xq(i):
                wait(act, xn_done, i)
                act.dma_start(xq[0:PW, :], a["x"][bass.ds(i * PW, PW), :]).then_inc(xq_in, 16)

            def load_xr(i):
                wait(act, x1_done, i)
                act.dma_start(xr[0:PW, :], a["x"][bass.ds(i * PW, PW), :]).then_inc(xr_in, 16)

            def store_x1(i):
                act.wait_ge(x1_done, i + 1)
                act.dma_start(x1_dram[bass.ds(i * PW, PW), :], x1[0:PW, :]).then_inc(x1_out, 16)

            def second_of_two(part):
                cols = slice(0, RT) if part == 0 else slice(RT, NT)
                act.wait_ge(diff_done, part + 1)
                act.activation(e21[:, cols], e21[:, cols], ACT.Exp).then_inc(e21_done, 1)

            def pair(i, first=False, final=False):
                for c in range(PC):
                    q, j = divmod(c, GC)
                    if c == 0 and not final:
                        load_xq(i + 1)
                    exps(i, c)
                    if j < KD and not (final and q == PG - 1):
                        k_hi_evac(i * PG + q + 1, j, (q + 1) % 2)
                    if (q, j) == (0, 2) and not first:
                        sums_spread(i - 1)
                    if (q, j) == (0, 3):
                        expert_hi(i)
                    if (q, j) == (1, 2) and not final:
                        x_transposed(i + 1)
                    if (q, j) == (5, 0):
                        if not first:
                            store_x1(i - 1)
                        load_xr(i)
                        if not final:
                            load_matrix(i + 1)
                    if (q, j) == (5, 1) and not first:
                        y_transposed(i - 1)
                    if (q, j) == (5, 3) and final:
                        second_of_two(0)

            act.dma_start(xq[0:PW, :], a["x"][0:PW, :]).then_inc(xq_in, 16)
            act.dma_start(wk[:, :, :], a["wk"]).then_inc(wk_in, 16)
            act.dma_start(wq[:, :, :], a["wq"]).then_inc(wq_in, 16)
            act.dma_start(rowv[:, :], bcast(a["rows"], P)).then_inc(row_in, 16)
            x_transposed(0, first_side)
            for src, dst, arrived in ((wk, wk_hi, wk_in), (wv, wv_hi, wv_in)):
                act.wait_ge(arrived, 16)
                act.activation(dst[:, :, :], src[:, :, :], ACT.Copy).then_inc(whi_done, 1)
            act.wait_ge(row_in, 16)
            act.activation(tg[:, :], gates[:, 0:2], ACT.Tanh).then_inc(tanh_done, 1)
            load_matrix(0)
            act.wait_ge(cst_in, 16)
            for m in range(KD):
                k_hi_evac(0, m, 0)
            act.wait_ge(m_ready, 2)
            pair(0, first=True)
            with act.Fori(1, NP - 1) as i:
                pair(i)
            pair(NP - 1, final=True)

            def hidden(f, first=False):
                for e in range(NE):
                    u = f * NE + e
                    at = step(f, e)
                    act.wait_ge(fc_done, u + 1)
                    if not (first and e < 2):
                        act.wait_ge(sq_done, u - 1)
                    act.activation(h_relu[:, e % 2, :, :], sc_ps[:, e % 2, :].rearrange("p (m n) -> p m n", m=KD),
                                   ACT.Relu).then_inc(relu_done, 1)
                    act.wait_ge(sq_done, u + 1)
                    if not (first and e < NB):
                        act.wait_ge(y2_done, u - NB + 1)
                    act.activation(h_hi[:, e % NB, :, :], h_sq[:, e % 2, :, :], ACT.Copy).then_inc(hhi_done, 1)
                    if at == 0:
                        sums_spread(NP - 1)
                    if at == 7:
                        store_x1(NP - 1)
                    if at == 9:
                        y_transposed(NP - 1)
                    if at == 15:
                        second_of_two(1)

            hidden(0, first=True)
            hidden(1)
            with act.Fori(2, NF) as f:
                hidden(f)
            act.wait_ge(x1_out, 16 * NP)

        @block.vector
        def _(dve):
            seq = [0]

            def then(ins):
                seq[0] += 1
                ins.then_inc(dve_seq, 1)
                dve.wait_ge(dve_seq, seq[0])

            def statistics(ln, i, src):
                dve.bn_stats(st6[ln][0:PW, :], src[0:PW, :]).then_inc(ln_step[ln], 1)
                dve.wait_ge(ln_step[ln], 2 * i + 1)
                dve.memset(held[ln][:, :], 0.0)
                dve.bn_aggr(mv[ln][0:PW, :], st6[ln][0:PW, :]).then_inc(ln_step[ln], 1)
                dve.wait_ge(ln_step[ln], 2 * i + 2)
                dve.tensor_scalar(var_e[ln][0:PW, :], mv[ln][0:PW, 1:2], EPS, None, ALU.add).then_inc(var_done[ln], 1)

            def normalised(ln, i, dst, src):
                dve.wait_ge(rstd_done[ln], i + 1)
                return dve.tensor_scalar(dst[0:PW, :], src[0:PW, :], mv[ln][0:PW, 0:1], rstd[ln][0:PW, :],
                                         ALU.subtract, ALU.mult)

            def k_lo_evac(n, m, s):
                for half in range(2):
                    dve.wait_ge(k_hi, 2 * KD * n + 2 * m + half + 1)
                    rows, other = slice(half * 64, half * 64 + 64), slice(64 - half * 64, 128 - half * 64)
                    dve.scalar_tensor_tensor(kst[other, s, 2 * m + half, :], k_ps[rows, m, 0:TG], bk[rows, m:m + 1],
                                             plain(kst[rows, s, 2 * m + half, :]), ALU.add, ALU.subtract).then_inc(k_lo, 1)

            def v_evac_step(n, j, s):
                dve.wait_ge(vproj_done, n * GC + j + 1)
                wait(dve, pv_done, (n - 2) * GC + j + 1)
                dve.tensor_tensor(vst[0:TC, s, j, :, 0:HD], v_bank(n, j)[0:TC, 0:D].rearrange("p (h d) -> p h d", h=NH),
                                  bv[0:TC, :].rearrange("p (h d) -> p h d", h=NH), ALU.add).then_inc(v_evac, 1)

            def q_evac(i, bank=side_ps):
                dve.wait_ge(qp_done, i + 1)
                wait(dve, q_step, 4 * i)
                for half in range(2):
                    src = slice(half * HW, (half + 1) * HW)
                    for copy in range(2):
                        dve.tensor_tensor(qT[copy * HW:(copy + 1) * HW, half:ST:2, :],
                                          bank[src, 0:KD * PW].rearrange("p (m n) -> p m n", m=KD),
                                          bq[src, :].unsqueeze(2).to_broadcast([HW, KD, PW]), ALU.add).then_inc(qT_done, 1)

            def q_split(i, b):
                n = 2 * i + b
                src = qT[:, :, b * S:(b + 1) * S]
                dve.wait_ge(qT_done, 4 * (i + 1))
                wait(dve, q_ready, 2 * n)
                dve.tensor_copy(q_rnd[:, :, :], src).then_inc(q_step, 1)
                dve.wait_ge(q_step, 2 * n + 1)
                dve.tensor_tensor(q_rem[:, :, :], src, plain(q_rnd[:, :, :]), ALU.subtract).then_inc(q_step, 1)

            def q_high(i, b):
                n = 2 * i + b
                dve.wait_ge(q_step, 2 * n + 2)
                wait(dve, scores_done, NC * (n - 1))
                q_diagonal(q_hi, b, plain(q_rnd[:, :, :]))

            def q_low(i, b):
                dve.wait_ge(q_step, 2 * (2 * i + b) + 2)
                q_diagonal(q_lo, b, q_rem[:, :, :])

            def q_diagonal(dst, b, part):
                shape = [P, ST, HS, S]
                dve.tensor_tensor(dst[:, b, :, :, :], part.unsqueeze(2).to_broadcast(shape),
                                  hmask[:, :].unsqueeze(1).unsqueeze(3).to_broadcast(shape), ALU.mult).then_inc(q_ready, 1)

            def o_evac_step(i, b):
                dve.wait_ge(pv_done, NC * (2 * i + b + 1))
                if b == 0:
                    wait(dve, norm_done, i)
                dve.tensor_copy(ctxo[:, :, b * S:(b + 1) * S],
                                o_ps[:, 0:ST * S].rearrange("p (c n) -> p c n", c=ST)).then_inc(o_evac, 1)

            def sums_split(i, b):
                n, cols = 2 * i + b, slice(b * S, (b + 1) * S)
                dve.wait_ge(o_evac, n + 1)
                wait(dve, sum_done, i)
                dve.tensor_copy(sum_hi[:, :, cols], ctxo[:, :, cols]).then_inc(sum_split, 1)
                dve.wait_ge(sum_split, 2 * n + 1)
                dve.tensor_tensor(sum_lo[:, :, cols], ctxo[:, :, cols], plain(sum_hi[:, :, cols]),
                                  ALU.subtract).then_inc(sum_split, 1)

            def inverse(i, col):
                dve.wait_ge(sum_evac, i + 1)
                dve.reciprocal(rec[:, col, :], rec[:, col, :]).then_inc(rec_done, 1)

            def divide(i):
                dve.wait_ge(rec_done, ST * (i + 1))
                dve.tensor_tensor(rec[:, :, :], ctxo[:, :, :], rec[:, :, :], ALU.mult).then_inc(norm_done, 1)

            def delta(i):
                dve.wait_ge(op_done, i + 1)
                dve.scalar_tensor_tensor(dlt[0:PW, :], side_ps[0:PW, 0:D], rs[0:PW, 0:1], bo[0:PW, :],
                                         ALU.mult, ALU.add).then_inc(dlt_evac, 1)

            def delta_statistics(i):
                dve.wait_ge(dlt_evac, i + 1)
                statistics(1, i, dlt)

            def x_after(i):
                normalised(1, i, dlt, dlt).then_inc(x1_step, 1)
                dve.wait_ge(x1_step, 2 * i + 1)
                dve.tensor_tensor(dlt[0:PW, :], dlt[0:PW, :], gam[0:PW, :], ALU.mult).then_inc(x1_step, 1)
                dve.wait_ge(x1_step, 2 * i + 2)
                dve.wait_ge(xb_done, i + 1)
                wait(dve, x1_out, 16 * i)
                dve.tensor_tensor(x1[0:PW, :], dlt[0:PW, :], xr[0:PW, :], ALU.add).then_inc(x1_done, 1)

            def x_after_statistics(i):
                dve.wait_ge(x1_done, i + 1)
                statistics(2, i, x1)

            def y_low(i):
                dve.wait_ge(yhi_done, i + 1)
                dve.tensor_tensor(yT_lo[:, :, bass.ds(i * PW, PW)], side_ps[:, 0:KD * PW].rearrange("p (k n) -> p k n", k=KD),
                                  plain(yT_hi[:, :, bass.ds(i * PW, PW)]), ALU.subtract).then_inc(ylo_done, 1)

            def route_parts(part):
                t0, t1 = (0, RT) if part == 0 else (RT, NT)
                shape = [P, t1 - t0, NE]
                revs = rev_e[:, :].unsqueeze(1).to_broadcast(shape)
                return t0, t1, revs, (lambda b: b[:, t0:t1].unsqueeze(2).to_broadcast(shape))

            def route_largest(part, top, pick):
                t0, t1, revs, over_e = route_parts(part)
                lg, ht = logit[:, t0:t1, :], hit[:, t0:t1, :]
                if top is top1:
                    dve.wait_ge(lg_done, t1)
                    both = logit_ps[part][:, t0 * 2 * NE:t1 * 2 * NE].rearrange("p (t r e) -> p t r e", r=2, e=NE)
                    then(dve.tensor_copy(lg, both[:, :, 0, :]))
                    then(dve.tensor_tensor(lg, lg, both[:, :, 1, :], ALU.add))
                else:
                    then(dve.scalar_tensor_tensor(lg, pick1[:, t0:t1, :], -BIG, lg, ALU.mult, ALU.add))
                then(dve.tensor_reduce(top[:, t0:t1], lg, AX.X, ALU.max))
                then(dve.tensor_tensor(ht, lg, over_e(top), ALU.is_equal))
                then(dve.tensor_tensor(ht, ht, revs, ALU.mult))
                then(dve.tensor_reduce(firstof[:, t0:t1], ht, AX.X, ALU.max))
                then(dve.tensor_tensor(pick[:, t0:t1, :], revs, over_e(firstof), ALU.is_equal))
                if top is top2:
                    dve.tensor_tensor(e21[:, t0:t1], top2[:, t0:t1], top1[:, t0:t1], ALU.subtract).then_inc(diff_done, 1)

            def route_weights(part):
                t0, t1, _, over_e = route_parts(part)
                p1, p2 = pick1[:, t0:t1, :], pick2[:, t0:t1, :]
                dve.wait_ge(e21_done, part + 1)
                then(dve.tensor_scalar(pr2[:, t0:t1], e21[:, t0:t1], 1.0, None, ALU.add))
                then(dve.reciprocal(pr1[:, t0:t1], pr2[:, t0:t1]))
                then(dve.tensor_scalar(pr1[:, t0:t1], pr1[:, t0:t1], tg[:, 1:2], None, ALU.mult))
                then(dve.tensor_tensor(pr2[:, t0:t1], pr1[:, t0:t1], e21[:, t0:t1], ALU.mult))
                dve.tensor_tensor(p1, p1, over_e(pr1), ALU.mult)
                then(dve.tensor_tensor(p2, p2, over_e(pr2), ALU.mult))
                then(dve.tensor_tensor(w_tok[:, t0:t1, :], p1, p2, ALU.add))

            def pair(i, first=False, final=False):
                for c in range(PC):
                    q, j = divmod(c, GC)
                    n = i * PC + c
                    more = not (final and q == PG - 1)
                    if more and j >= KD:
                        v_evac_step(i * PG + q + 1, j, (q + 1) % 2)
                    dve.wait_ge(exp_done, n + 1)
                    p = prob[0:TC, c % PB, :]
                    dve.tensor_scalar(p, p, EXP_LO, EXP_HI, ALU.max, ALU.min).then_inc(clip_done, 1)
                    if more and j < KD:
                        v_evac_step(i * PG + q + 1, j, (q + 1) % 2)
                        k_lo_evac(i * PG + q + 1, j, (q + 1) % 2)
                    beside(i, q, j, first, final)

            def beside(i, q, j, first, final):
                at = (q, j)
                if at == (0, 0):
                    q_split(i, 1)
                    if not first:
                        o_evac_step(i - 1, 1)
                        sums_split(i - 1, 1)
                if at == (0, 3):
                    if not final:
                        dve.wait_ge(xq_in, 16 * (i + 2))
                        statistics(0, i + 1, xq)
                    q_high(i, 1)
                    if not first:
                        inverse(i - 1, 0)
                if at == (1, 0) and not final:
                    normalised(0, i + 1, xn, xq).then_inc(xn_done, 1)
                if at == (1, 2):
                    q_low(i, 1)
                    if not first:
                        inverse(i - 1, 1)
                        inverse(i - 1, 2)
                if at == (2, 1) and not first:
                    inverse(i - 1, 3)
                    divide(i - 1)
                if at == (2, 2) and not final:
                    q_evac(i + 1)
                if at == (3, 0) and not final:
                    q_split(i + 1, 0)
                if at == (3, 1):
                    o_evac_step(i, 0)
                if at == (4, 2):
                    sums_split(i, 0)
                if at == (3, 2) and not first:
                    delta(i - 1)
                if at == (3, 3):
                    if not first:
                        delta_statistics(i - 1)
                    if not final:
                        q_high(i + 1, 0)
                if at == (4, 2) and not first:
                    x_after(i - 1)
                    x_after_statistics(i - 1)
                if at == (5, 0) and not first:
                    normalised(2, i - 1, dlt, x1).then_inc(y_done, 1)
                if at == (5, 1):
                    if not final:
                        q_low(i + 1, 0)
                    if not first:
                        y_low(i - 1)
                if final and at == (5, 0):
                    route_largest(0, top1, pick1)
                if final and at == (5, 1):
                    route_largest(0, top2, pick2)
                if final and at == (5, 3):
                    route_weights(0)

            dve.wait_ge(xq_in, 16)
            statistics(0, 0, xq)
            normalised(0, 0, xn, xq).then_inc(xn_done, 1)
            for i, (src, hi, lo) in enumerate(((wk, wk_hi, wk_lo), (wv, wv_hi, wv_lo))):
                dve.wait_ge(whi_done, i + 1)
                dve.tensor_tensor(lo[:, :, :], src[:, :, :], plain(hi[:, :, :]), ALU.subtract).then_inc(wlo_done, 1)
            dve.wait_ge(cst_in, 16)
            q_evac(0, first_side)
            q_split(0, 0)
            q_high(0, 0)
            q_low(0, 0)
            dve.wait_ge(mask_in, 16)
            dve.tensor_scalar(m_scale[0:TC, :], mask_i[0:TC, :], 0.5, SCALE, ALU.is_gt, ALU.mult).then_inc(m_ready, 1)
            dve.wait_ge(m_ready, 1)
            dve.tensor_scalar(m_bias[0:TC, :], m_scale[0:TC, :], CLIP / SCALE, -CLIP, ALU.mult, ALU.add).then_inc(m_ready, 1)
            dve.wait_ge(row_in, 16)
            dve.wait_ge(ones_done, 3)
            dve.tensor_copy(sumsel_r[:, :], sumsel[:, :]).then_inc(sel_done, 1)
            for m in range(KD):
                k_lo_evac(0, m, 0)
            for j in range(GC):
                v_evac_step(0, j, 0)
            dve.wait_ge(v_evac, GC)
            dve.memset(o_ps[:, :], 0.0).then_inc(o_clear, 1)
            dve.wait_ge(tanh_done, 1)
            dve.tensor_scalar(rs[:, :], gates[:, 2:3], 0.0, RES_SCALE_MAX, ALU.max, ALU.min).then_inc(scale_done, 1)
            dve.wait_ge(scale_done, 1)
            for t, by in ((bo, rs[:, 0:1]), (gam, tg[:, 0:1]), (bet, tg[:, 0:1])):
                dve.tensor_scalar(t[:, :], t[:, :], by, None, ALU.mult).then_inc(scale_done, 1)
            dve.wait_ge(wr_split, 16)
            dve.tensor_copy(wr_2[:, :, 0, :], wr[:, :, :]).then_inc(wr_split, 1)
            dve.wait_ge(wr_split, 17)
            dve.tensor_tensor(wr_2[:, :, 1, :], wr[:, :, :], plain(wr_2[:, :, 0, :]), ALU.subtract).then_inc(wr_split, 1)
            dve.wait_ge(scale_done, 4)
            pair(0, first=True)
            with dve.Fori(1, NP - 1) as i:
                pair(i)
            pair(NP - 1, final=True)

            def accumulate(f, e):
                u = f * NE + e
                dve.wait_ge(y2_done, u + 1)
                for t in range(2):
                    tile = f * 2 + t
                    if e > 0:
                        dve.wait_ge(acc_done, 2 * u - 1 + t)
                    total = acc[:, bass.ds(tile, 1), :].squeeze(1)
                    dve.scalar_tensor_tensor(total, sc_ps[:, 2 + e % 2, t * D:(t + 1) * D],
                                             w_tok[:, bass.ds(tile, 1), e], total, ALU.mult, ALU.add).then_inc(acc_done, 1)

            def experts(f, first=False):
                for e in range(NE):
                    u = f * NE + e
                    dve.wait_ge(relu_done, u + 1)
                    if not (first and e < 2):
                        dve.wait_ge(hlo_done, u - 1)
                    r = h_relu[:, e % 2, :, :]
                    dve.tensor_tensor(h_sq[:, e % 2, :, :], r, r, ALU.mult).then_inc(sq_done, 1)
                    if e >= 2:
                        accumulate(f, e - 2)
                    elif not first:
                        accumulate(f - 1, NE - 2 + e)
                    beside_experts(step(f, e))

            def beside_experts(at):
                if at == 0:
                    o_evac_step(NP - 1, 1)
                    sums_split(NP - 1, 1)
                    inverse(NP - 1, 0)
                    inverse(NP - 1, 1)
                if at == 1:
                    inverse(NP - 1, 2)
                    inverse(NP - 1, 3)
                    divide(NP - 1)
                    dve.wait_ge(acc_in[0], 16)
                if at == 5:
                    delta(NP - 1)
                    delta_statistics(NP - 1)
                if at == 6:
                    x_after(NP - 1)
                    x_after_statistics(NP - 1)
                if at == 7:
                    normalised(2, NP - 1, dlt, x1).then_inc(y_done, 1)
                    dve.wait_ge(acc_in[1], 16)
                if at == 10:
                    y_low(NP - 1)
                if at == 13:
                    route_largest(1, top1, pick1)
                if at == 14:
                    route_largest(1, top2, pick2)
                if at == 15:
                    route_weights(1)
                    dve.wait_ge(acc_in[2], 16)

            experts(0, first=True)
            experts(1)
            with dve.Fori(2, NF) as f:
                experts(f)
            accumulate(NF - 1, NE - 2)
            accumulate(NF - 1, NE - 1)


def kernel(x, ctx_2048, mask_BxS2_ik0, g_xattn, g_ffn, L0_xattn_Wq, L0_xattn_bq, L0_xattn_Wk, L0_xattn_bk,
           L0_xattn_Wv, L0_xattn_bv, L0_xattn_Wo, L0_xattn_bo, L0_xattn_ln_gamma, L0_xattn_ln_beta,
           L0_xattn_residual_scale, L0_ffn_w_router, L0_ffn_w_fc, L0_ffn_w_proj):
    import numpy as np
    import concourse.bacc as bacc
    from concourse.bass_utils import run_bass_kernel_spmd

    def rows(w):
        w = np.asarray(w)
        w = w.reshape(w.shape[:-2] + (KD, P, w.shape[-1]))
        return np.ascontiguousarray(np.moveaxis(w, -3, -2))

    def row(v):
        return np.ascontiguousarray(np.asarray(v).reshape(1, -1))

    ctxT = np.asarray(ctx_2048).reshape(B * NG, TG, KD, P).transpose(0, 3, 2, 1)
    wo = np.ascontiguousarray(np.asarray(L0_xattn_Wo).T.reshape(KD, 2, ST, HD, D).transpose(2, 1, 3, 0, 4))
    r = np.arange(P)
    arrays = {
        "x": np.ascontiguousarray(np.asarray(x).reshape(TOK, D)),
        "ctxT": np.ascontiguousarray(ctxT),
        "mask": np.ascontiguousarray(np.asarray(mask_BxS2_ik0).reshape(B * NC, TC).T),
        "wk": rows(np.asarray(L0_xattn_Wk).T), "wv": rows(np.asarray(L0_xattn_Wv).T), "wq": rows(np.asarray(L0_xattn_Wq).T),
        "wo": wo.reshape(P, KD, D), "wr": rows(L0_ffn_w_router),
        "we": np.ascontiguousarray(np.stack([rows(L0_ffn_w_fc), rows(L0_ffn_w_proj)], 1).reshape(NW, P, KD, D)),
        "rows": np.concatenate([row(v) for v in (L0_xattn_bv, L0_xattn_bo, L0_xattn_ln_gamma, L0_xattn_ln_beta,
                                                 g_xattn, g_ffn, L0_xattn_residual_scale)], 1),
        "cst": np.ascontiguousarray(np.concatenate([
            np.eye(P, dtype=np.float32),
            (r[:, None] == r[None, :] // 32 * 32 + HD).astype(np.float32),
            np.tile(NE - np.arange(NE, dtype=np.float32), (P, 1)),
            (r[:, None] % HW // HD == np.arange(HS)[None, :]).astype(np.float32),
            np.asarray(L0_xattn_bk).reshape(KD, P).T, np.asarray(L0_xattn_bq).reshape(KD, P).T], 1)),
    }
    nc = bacc.Bacc("TRN2", target_bir_lowering=False, num_devices=1)
    args = {k: nc.dram_tensor(f"in_{k}", v.shape, mybir.dt.from_np(v.dtype), kind="ExternalInput").ap()
            for k, v in arrays.items()}
    out = nc.dram_tensor("out_y", (P, NT, D), mybir.dt.float32, kind="ExternalOutput").ap()
    x1_dram = nc.dram_tensor("x1_scratch", (TOK, D), mybir.dt.float32, kind="Internal").ap()
    gated_cross_attention_moe(nc, args, x1_dram, out)
    got = run_bass_kernel_spmd(nc, [{f"in_{k}": v for k, v in arrays.items()}], core_ids=[0])
    y = got.results[0]["out_y"]
    return np.ascontiguousarray(y.transpose(1, 0, 2)).reshape(B, S, D)
```
